# Optimizing a Trainium2 kernel written in Bass

```python
import numpy as np
import jax
import jax.numpy as jnp

def _softmax(x, axis=-1):
    return jax.nn.softmax(x, axis=axis)
def _gelu(x):
    return jax.nn.gelu(x, approximate=True)
def _silu(x):
    return jax.nn.silu(x)
def _sigmoid(x):
    return jax.nn.sigmoid(x)
def _layernorm(x, axis=-1, eps=1e-5):
    m = jnp.mean(x, axis=axis, keepdims=True)
    v = jnp.var(x, axis=axis, keepdims=True)
    return (x - m) / jnp.sqrt(v + eps)
def _scatter_add(tgt, idx, src, axis=0):
    return tgt.at[idx].add(src)
def _segment_sum(src, seg, n):
    return jax.ops.segment_sum(src, seg, n)

kernel_name = 'mk_conv_preact_d2_conv_nchw512_9ce20b'

def setup_inputs(seed: int = 0):
    np.random.seed(seed)
    _w = jnp.asarray
    def _rec_inputs():
        import jax
        import jax.numpy as jnp
        _gk = jax.random.key(seed)
        x = -7.109e-05 + 0.9999 * jax.random.normal(jax.random.fold_in(_gk, 1), (8, 512, 128, 128), jnp.float32)
        return x
    x = _rec_inputs()
    def _L0_conv_setup():
        import jax, jax.numpy as jnp
        import numpy as np
        NUM_HEADS = 8
        IN_C = 64
        C_M = 64
        C_N = 64
        key = jax.random.key(seed)
        k = jax.random.split(key, 7)
        B, H, W = (8, 128, 128)
        x = jax.random.normal(k[0], (B, NUM_HEADS * IN_C, H, W), dtype=jnp.float32)
        s = 1.0 / np.sqrt(IN_C)
        Wa = jax.random.uniform(k[1], (C_M, IN_C), jnp.float32, -s, s)
        ba = jax.random.uniform(k[2], (C_M,), jnp.float32, -s, s)
        Wb = jax.random.uniform(k[3], (C_N, IN_C), jnp.float32, -s, s)
        bb = jax.random.uniform(k[4], (C_N,), jnp.float32, -s, s)
        Wv = jax.random.uniform(k[5], (C_N, IN_C), jnp.float32, -s, s)
        bv = jax.random.uniform(k[6], (C_N,), jnp.float32, -s, s)
        return {'x': x, 'Wa': Wa, 'ba': ba, 'Wb': Wb, 'bb': bb, 'Wv': Wv, 'bv': bv}
    _L0_conv_all = _L0_conv_setup()
    _L0_conv_in = {k: v for k, v in _L0_conv_all.items() if k in ('Wa', 'ba', 'Wb', 'bb', 'Wv', 'bv', )}
    del _L0_conv_all

    def _L1_conv_setup():
        import jax, jax.numpy as jnp
        from jax import lax
        import numpy as np
        UP = 2
        DOWN = 2
        PADDING = (11, 10, 11, 10)
        GAIN = float(np.sqrt(2.0))
        SLOPE = 0.2
        CLAMP = 256.0
        UP_TAPS = 12
        IN_CUTOFF = 8.0
        OUT_CUTOFF = 8.0
        IN_HALF_WIDTH = 6.0
        OUT_HALF_WIDTH = 6.0
        TEMP_FS = 32.0

        def _design_lowpass(numtaps, cutoff, width, fs):
            nyq = fs / 2.0
            atten = 2.285 * (numtaps - 1) * np.pi * (width / nyq) + 7.95
            if atten > 50.0:
                beta = 0.1102 * (atten - 8.7)
            elif atten > 21.0:
                beta = 0.5842 * (atten - 21.0) ** 0.4 + 0.07886 * (atten - 21.0)
            else:
                beta = 0.0
            m = np.arange(numtaps) - (numtaps - 1) / 2.0
            c = cutoff / nyq
            h = c * np.sinc(c * m)
            h = h * np.kaiser(numtaps, beta)
            h = h / np.sum(h)
            return h.astype(np.float32)

        def _upfirdn2d_sep(x, f, up, down, pad, gain):
            N, C, H, W = x.shape
            fr = f[::-1].astype(x.dtype)
            kH = fr.reshape(1, 1, -1, 1)
            kW = fr.reshape(1, 1, 1, -1)
            px0, px1, py0, py1 = pad
            xr = x.reshape(N * C, 1, H, W)
            xr = lax.conv_general_dilated(xr, kH, window_strides=(down, 1), padding=((py0, py1 + up - 1), (0, 0)), lhs_dilation=(up, 1))
            xr = lax.conv_general_dilated(xr, kW, window_strides=(1, down), padding=((0, 0), (px0, px1 + up - 1)), lhs_dilation=(1, up))
            Ho, Wo = (xr.shape[2], xr.shape[3])
            return xr.reshape(N, C, Ho, Wo) * gain
        key = jax.random.key(seed)
        k1, k2 = jax.random.split(key)
        x = jax.random.normal(k1, (8, 512, 64, 64), dtype=jnp.float32)
        bias = jax.random.normal(k2, (512,), dtype=jnp.float32) * 0.1
        up_filter = jnp.asarray(_design_lowpass(UP_TAPS, IN_CUTOFF, IN_HALF_WIDTH * 2, TEMP_FS))
        down_filter = jnp.asarray(_design_lowpass(UP_TAPS, OUT_CUTOFF, OUT_HALF_WIDTH * 2, TEMP_FS))
        return {'x': x, 'bias': bias, 'up_filter': up_filter, 'down_filter': down_filter}
    _L1_conv_all = _L1_conv_setup()
    _L1_conv_in = {k: v for k, v in _L1_conv_all.items() if k in ('bias', 'up_filter', 'down_filter', )}
    del _L1_conv_all

    return {
        "x": x,
        "L0_conv_Wa": _L0_conv_in["Wa"],
        "L0_conv_ba": _L0_conv_in["ba"],
        "L0_conv_Wb": _L0_conv_in["Wb"],
        "L0_conv_bb": _L0_conv_in["bb"],
        "L0_conv_Wv": _L0_conv_in["Wv"],
        "L0_conv_bv": _L0_conv_in["bv"],
        "L1_conv_bias": _L1_conv_in["bias"],
        "L1_conv_up_filter": _L1_conv_in["up_filter"],
        "L1_conv_down_filter": _L1_conv_in["down_filter"],
    }

def reference(x, L0_conv_Wa, L0_conv_ba, L0_conv_Wb, L0_conv_bb, L0_conv_Wv, L0_conv_bv, L1_conv_bias, L1_conv_up_filter, L1_conv_down_filter):
    import jax
    import jax.numpy as jnp
    def _L0_conv_ref(x, Wa, ba, Wb, bb, Wv, bv):
        import jax, jax.numpy as jnp
        import numpy as np
        NUM_HEADS = 8
        IN_C = 64
        C_M = 64
        C_N = 64
        B, C, Hh, Ww = x.shape
        S = Hh * Ww
        xh = x.reshape(B, NUM_HEADS, IN_C, S)
        A = jnp.einsum('mi,bhis->bhms', Wa, xh) + ba[:, None]
        Bm = jnp.einsum('ni,bhis->bhns', Wb, xh) + bb[:, None]
        V = jnp.einsum('ni,bhis->bhns', Wv, xh) + bv[:, None]
        attn_maps = jax.nn.softmax(Bm, axis=-1)
        attn_vecs = jax.nn.softmax(V, axis=2)
        G = jnp.einsum('bhms,bhns->bhmn', A, attn_maps)
        Z = jnp.einsum('bhmn,bhns->bhms', G, attn_vecs)
        return Z.reshape(B, NUM_HEADS * C_M, Hh, Ww)

    def _L1_conv_ref(x, bias, up_filter, down_filter):
        import jax, jax.numpy as jnp
        from jax import lax
        import numpy as np
        UP = 2
        DOWN = 2
        PADDING = (11, 10, 11, 10)
        GAIN = float(np.sqrt(2.0))
        SLOPE = 0.2
        CLAMP = 256.0
        UP_TAPS = 12
        IN_CUTOFF = 8.0
        OUT_CUTOFF = 8.0
        IN_HALF_WIDTH = 6.0
        OUT_HALF_WIDTH = 6.0
        TEMP_FS = 32.0

        def _design_lowpass(numtaps, cutoff, width, fs):
            nyq = fs / 2.0
            atten = 2.285 * (numtaps - 1) * np.pi * (width / nyq) + 7.95
            if atten > 50.0:
                beta = 0.1102 * (atten - 8.7)
            elif atten > 21.0:
                beta = 0.5842 * (atten - 21.0) ** 0.4 + 0.07886 * (atten - 21.0)
            else:
                beta = 0.0
            m = np.arange(numtaps) - (numtaps - 1) / 2.0
            c = cutoff / nyq
            h = c * np.sinc(c * m)
            h = h * np.kaiser(numtaps, beta)
            h = h / np.sum(h)
            return h.astype(np.float32)

        def _upfirdn2d_sep(x, f, up, down, pad, gain):
            N, C, H, W = x.shape
            fr = f[::-1].astype(x.dtype)
            kH = fr.reshape(1, 1, -1, 1)
            kW = fr.reshape(1, 1, 1, -1)
            px0, px1, py0, py1 = pad
            xr = x.reshape(N * C, 1, H, W)
            xr = lax.conv_general_dilated(xr, kH, window_strides=(down, 1), padding=((py0, py1 + up - 1), (0, 0)), lhs_dilation=(up, 1))
            xr = lax.conv_general_dilated(xr, kW, window_strides=(1, down), padding=((0, 0), (px0, px1 + up - 1)), lhs_dilation=(1, up))
            Ho, Wo = (xr.shape[2], xr.shape[3])
            return xr.reshape(N, C, Ho, Wo) * gain
        y = _upfirdn2d_sep(x, up_filter, UP, 1, PADDING, float(UP * UP))
        y = y + bias[None, :, None, None]
        y = jnp.where(y >= 0, y, y * SLOPE) * GAIN
        y = jnp.clip(y, -CLAMP, CLAMP)
        y = _upfirdn2d_sep(y, down_filter, 1, DOWN, (0, 0, 0, 0), 1.0)
        return y

    def _gn(v, G=32, eps=1e-5):
        B_, C_, H_, W_ = v.shape
        g = v.reshape(B_, G, C_ // G, H_, W_)
        m = jnp.mean(g, axis=(2, 3, 4), keepdims=True)
        s = jnp.var(g, axis=(2, 3, 4), keepdims=True)
        return ((g - m) / jnp.sqrt(s + eps)).reshape(v.shape)

    def _ln_c(v, eps=1e-6):
        m = jnp.mean(v, axis=1, keepdims=True)
        s = jnp.var(v, axis=1, keepdims=True)
        return (v - m) / jnp.sqrt(s + eps)

    def _ln_t(v, eps=1e-5):
        m = jnp.mean(v, axis=-1, keepdims=True)
        s = jnp.var(v, axis=-1, keepdims=True)
        return (v - m) / jnp.sqrt(s + eps)

    def _to_tokens(v):
        B_, C_, H_, W_ = v.shape
        return v.reshape(B_, C_, H_ * W_).transpose(0, 2, 1)
    def _from_tokens(t, like):
        B_, C_, H_, W_ = like.shape
        return t.transpose(0, 2, 1).reshape(B_, C_, H_, W_)

    x = x + _L0_conv_ref(_gn(x), L0_conv_Wa, L0_conv_ba, L0_conv_Wb, L0_conv_bb, L0_conv_Wv, L0_conv_bv)
    x = x + _L1_conv_ref(_gn(x), L1_conv_bias, L1_conv_up_filter, L1_conv_down_filter)
    return x


_drawn_inputs = setup_inputs


def setup_inputs(seed=0):
    import zlib

    import numpy as np

    out = dict(_drawn_inputs(seed))
    spreads = {}
    factors = {'L0_conv_Wa': 6.629,
     'L0_conv_Wb': 8.0,
     'L0_conv_bb': 8.0,
     'L0_conv_Wv': 8.0,
     'L0_conv_bv': 8.0}
    for name, (base, spread) in spreads.items():
        noise = np.random.default_rng([zlib.crc32(name.encode()), seed]).standard_normal(out[name].shape)
        drawn = base * np.exp(spread * noise) if base else spread * noise
        out[name] = jnp.asarray(drawn.astype(out[name].dtype))
    for name, factor in factors.items():
        out[name] = (out[name] * factor).astype(out[name].dtype)
    return out
```

```python
import concourse.bass as bass
from concourse import mybir
from contextlib import ExitStack

B, C, H, W = 8, 512, 128, 128
P = 128
HEAD = 64
HPU = P // HEAD
UNITS = B * C // P
CPB = C // P
GROUP = C // 32
NG = P // GROUP
EPS = 1e-5
WB = 4
NBLK = W // WB
BS = WB * H
XCH = 4
IMG = 8
NBAT = P // IMG
HALF = IMG // 2
TAPS = 12
UP = 2 * H + 10
REM = UP - 2 * P
RR = IMG * REM
DA, DB = 64, 69
DB0 = H - DB
DR = 5
SLOPE, CLAMP = 0.2, 256.0
GAIN = 2.0 ** 0.5
UPGAIN = 4.0
BIG = 3.0e38
N_SMALL = 22


def attention_then_filters(nc, x, WaT, ba, WbT, bb_, WvT, bv, bias, fup, fdn, out):
    fp32, bf16 = mybir.dt.float32, mybir.dt.bfloat16
    ALU, ACT, AX = mybir.AluOpType, mybir.ActivationFunctionType, mybir.AxisListType

    x_ch = x.rearrange("b (u c) h w -> (b u) c (h w)", c=P)
    x_row = x.rearrange("b (u c) h w -> (b u) h c w", c=P)
    out_row = out.rearrange("b (u c) h w -> (b u) h c w", c=P)

    ctx = ExitStack()
    with ctx:
        def sb(name, shape, dt=fp32):
            return ctx.enter_context(nc.sbuf_tensor(name, shape, dt))

        def pb(name, shape, dt=fp32):
            return ctx.enter_context(nc.psum_tensor(name, shape, dt))

        def sem(name):
            return ctx.enter_context(nc.semaphore(name))

        xc = sb("xc", [P, H * W])
        xh = sb("xh", [P, P, W])
        xc_wh = xc[:, :].rearrange("c (h w) -> c w h", w=W)
        xh_wc = xh[:, :, :].rearrange("h c w -> h w c")
        ident = sb("ident", [P, P])
        nident = sb("nident", [P, P], bf16)
        avg_c = sb("avg_c", [P, P])
        avg_p = sb("avg_p", [P, P])
        wa2 = sb("wa2", [P, P])
        wb2 = sb("wb2", [P, P])
        wv2 = sb("wv2", [P, P])
        ba_diag = sb("ba_diag", [P, P])
        bb_col = sb("bb_col", [P, 1])
        bv_col = sb("bv_col", [P, 1])
        bv_row = sb("bv_row", [1, P])
        bv_row4 = sb("bv_row4", [1, WB, P], bf16)
        ones_row = sb("ones_row", [1, P], bf16)
        up_t = sb("up_t", [P, UP])
        dn_t = sb("dn_t", [P, DB])
        dn_r = sb("dn_r", [RR, IMG, DR])
        dn_rs = sb("dn_rs", [RR, DR])
        own = sb("own", [RR, IMG])
        f_up = sb("f_up", [P, TAPS])
        f_dn = sb("f_dn", [P, TAPS])
        bias_b = sb("bias_b", [P, C])
        bias_r = sb("bias_r", [RR, C // IMG])
        wbs = sb("wbs", [P, P])
        wvs = sb("wvs", [P, P])
        wvh = sb("wvh", [P, P], bf16)
        bvs = sb("bvs", [P, 1])
        bbs = sb("bbs", [P, 1])
        stc = sb("stc", [P, NBLK, 6])
        mvc = sb("mvc", [P, 2])
        sc = sb("sc", [P, 12])
        m0, nm0, r0, nmr0, v0, t0 = (sc[:, i:i + 1] for i in range(6))
        nblk = sb("nblk", [P, 2])
        nrun = sb("nrun", [P, 2])
        bexp = sb("bexp", [P, 2])
        alpha = sb("alpha", [P, 2])
        sblk = sb("sblk", [P, 2])
        srun = sb("srun", [P, 1])
        rsum = sb("rsum", [P, 1])
        mrun = sb("mrun", [P, P])
        xbar = sb("xbar", [P, P])
        xbart = sb("xbart", [P, P])
        gaug = sb("gaug", [P, HPU, HEAD + 1])
        pe_ = [sb(f"p{i}", [P, BS]) for i in range(2)]
        pt_ = [sb(f"pt{i}", [P, BS]) for i in range(2)]
        xb_ = [sb(f"xb{i}", [P, WB, P], bf16) for i in range(2)]
        ev_ = pe_
        tmax = [sb(f"tmax{i}", [P, WB, HPU], bf16) for i in range(2)]
        tspr = [sb(f"tspr{i}", [P, WB, HPU, HEAD], bf16) for i in range(2)]
        rinv = sb("rinv", [P, WB, HPU])
        zs_ = [t[:, :].rearrange("p (w h m) -> p w h m", w=WB, h=HPU) for t in pt_]
        sth = sb("sth", [P, NG, 4, 6])
        mvh = sb("mvh", [P, NG, 2])
        m1 = sb("m1", [P, NG])
        r1 = sb("r1", [P, NG])
        v1 = sb("v1", [P, NG])
        xn = sb("xn", [P, 2, IMG, W])
        t1 = sb("t1", [P, 2, UP, IMG])
        yb = sb("yb", [P, 2, UP, IMG])
        yr = sb("yr", [RR, UP])
        yrb = sb("yrb", [RR, REM, IMG])
        z1 = sb("z1", [P, 2, 2, HALF, H])
        zr = sb("zr", [RR, H])

        ps = pb("ps", [P, 8, 512])
        b_ps = [ps[:, i, :] for i in (0, 1)]
        pt_ps = [ps[:, i, :] for i in (2, 3)]
        m_ps = ps[:, 4, 0:P]
        tiny = ps[:, 5, :]
        v_ps = b_ps
        z_ps = [ps[:, i:i + 2, :].rearrange("p b (w n) -> p (b w) n", w=2) for i in (2, 4)]
        vt_ps = [ps[:, i, :] for i in (6, 7)]
        y_ps = [ps[:, i:i + 2, 0:UP] for i in (0, 2)]
        dz_ps = ps[:, 4:6, :]
        s1_ps = ps[:, 6, :]
        o_ps = ps[:, 7, :]

        s_par = sem("parameters_loaded")
        s_zero = sem("zeros_set")
        s_mask = sem("masks_set")
        s_wz = sem("weights_zeroed")
        s_cst_dve = sem("constant_steps")
        s_cst = sem("constants_ready")
        s_xc = [sem(f"xc_piece{i}_loaded") for i in range(XCH)]
        s_xh = [sem(f"xh_loaded_{i}") for i in range(2)]
        s_st = [sem(f"out_stored_{i}") for i in range(2)]
        s_small = sem("vector_small_steps")
        s_gn0 = sem("norm0_stats_ready")
        s_gn0p = sem("norm0_averaged")
        s_var0 = sem("norm0_variance_ready")
        s_sq0 = sem("norm0_sqrt_ready")
        s_w = sem("scaled_weights_ready")
        s_bvp = sem("value_bias_product")
        s_b = sem("b_scores_in_psum")
        s_nblk = sem("block_max_ready")
        s_nm = sem("running_max_ready")
        s_p = sem("exp_b_ready")
        s_al = sem("alpha_ready")
        s_pt = sem("exp_b_transposed")
        s_ptc = sem("exp_b_transposed_copied")
        s_m = sem("block_sum_in_psum")
        s_ma = sem("block_sum_added")
        s_xbar = sem("xbar_ready")
        s_xbp = sem("xbar_transposed")
        s_xbt = sem("xbar_t_ready")
        s_gp = sem("g_in_psum")
        s_g = sem("g_ready")
        s_xb = sem("xc_bf16_ready")
        s_vt = sem("v_transposed_in_psum")
        s_t = sem("v_max_ready")
        s_ts = sem("v_max_spread")
        s_v = sem("v_in_psum")
        s_e = sem("exp_v_ready")
        s_zz = sem("z_in_psum")
        s_zn = sem("z_normalised")
        s_x1 = sem("x1_written")
        s_gn1 = sem("norm1_stats_ready")
        s_gn1p = sem("norm1_averaged")
        s_var1 = sem("norm1_variance_ready")
        s_sq1 = sem("norm1_sqrt_ready")
        s_xn = sem("xn_ready")
        s_s1 = sem("up_rows_in_psum")
        s_t1 = sem("up_rows_copied")
        s_yp = sem("up_2d_in_psum")
        s_y = sem("up_2d_scaled")
        s_lr = sem("leaky_relu_done")
        s_yc = sem("clipped")
        s_yrp = sem("remainder_rows_in_psum")
        s_yr = sem("remainder_rows_scaled")
        s_yrc = sem("remainder_rows_clipped")
        s_dz = sem("down_rows_in_psum")
        s_z1 = sem("down_rows_copied")
        s_zrp = sem("remainder_columns_in_psum")
        s_zr = sem("remainder_columns_copied")
        s_op = sem("output_in_psum")
        s_o = sem("output_added")

        ZCREDIT = 4
        s_alone = sem("lone_waits")

        ONE = 1
        YCREDIT = 2

        block = ctx.enter_context(nc.Block())

        def wait_alone(eng, semaphore, value):
            eng.wait_ge(semaphore, value)
            eng.sem_inc(s_alone, 1)

        def steps(eng, n, step):
            step(0, 0, False, True)
            step(1, 1, True, True)
            with eng.Fori(1, n // 2 - 1) as k:
                step(2 * k, 0, True, True)
                step(2 * k + 1, 1, True, True)
            step(n - 2, 0, True, True)
            step(n - 1, 1, True, False)

        @block.sync
        def _(sp):
            def load_xc(u):
                n = H * W // XCH
                for i in range(XCH):
                    sp.dma_start(xc[:, i * n:(i + 1) * n], x_ch[u, :, i * n:(i + 1) * n]).then_inc(s_xc[i], 16)

            def load_xh(u, j, par):
                sp.dma_start(xh[:, bass.ts(j, IMG), :], x_row[u, :, bass.ts(j, IMG), :]).then_inc(s_xh[par], 16)

            load_xc(0)
            sp.dma_start(f_up[:, :], fup.rearrange("(a n) -> a n", a=1).to_broadcast([P, TAPS])).then_inc(s_par, 16)
            sp.dma_start(f_dn[:, :], fdn.rearrange("(a n) -> a n", a=1).to_broadcast([P, TAPS])).then_inc(s_par, 16)
            sp.dma_start(bias_b[:, :], bias.rearrange("(a n) -> a n", a=1).to_broadcast([P, C])).then_inc(s_par, 16)
            sp.dma_start(bv_row[:, :].rearrange("a (t n) -> a t n", t=HPU),
                         bv.rearrange("(a t n) -> a t n", a=1, t=1).to_broadcast([1, HPU, HEAD])).then_inc(s_par, 16)
            sp.wait_ge(s_wz, 1)
            for h in range(HPU):
                d = slice(h * HEAD, (h + 1) * HEAD)
                for dst, src in ((wa2, WaT), (wb2, WbT), (wv2, WvT)):
                    sp.dma_start(dst[d, d], src).then_inc(s_par, 16)
                sp.dma_start(ba_diag[d, d], ba.rearrange("(a n) -> a n", a=1).to_broadcast([HEAD, HEAD])).then_inc(s_par, 16)
                sp.dma_start(bb_col[d, :], bb_.rearrange("(n a) -> n a", a=1)).then_inc(s_par, 16)
                sp.dma_start(bv_col[d, :], bv.rearrange("(n a) -> n a", a=1)).then_inc(s_par, 16)
            for i in range(REM):
                sp.dma_start(bias_r[i * IMG:(i + 1) * IMG, :], bias.rearrange("(t n) -> n t", n=IMG),
                             allow_slow_non_contiguous=True).then_inc(s_par, 16)
            for j in range(NBAT):
                load_xh(0, j, j % 2)

            def unit(u, more):
                if more:
                    wait_alone(sp, s_v, NBLK * (u + 1))
                    wait_alone(sp, s_xb, NBLK * (u + 1))
                    load_xc(u + 1)

                def batch(j, par, prev, nxt):
                    wait_alone(sp, s_o, 2 * (NBAT * u + j + 1) + ONE)
                    sp.dma_start(out_row[u, :, bass.ts(j, IMG), :], xh[:, bass.ts(j, IMG), :]).then_inc(s_st[par], 16)
                    if prev:
                        wait_alone(sp, s_st[1 - par], 16 * (NBAT // 2 * u + (j - 1) // 2 + 1))
                        if more:
                            load_xh(u + 1, j - 1, 1 - par)

                steps(sp, NBAT, batch)
                wait_alone(sp, s_st[1], 16 * (NBAT // 2 * (u + 1)))
                if more:
                    load_xh(u + 1, NBAT - 1, 1)

            with sp.Fori(0, UNITS - 1) as u:
                unit(u, True)
            unit(UNITS - 1, False)

        @block.gpsimd
        def _(pool):
            yflat = yb[:, :, :, :].rearrange("p a b c -> p (a b c)")
            tflat = t1[:, :, :, :].rearrange("p a b c -> p (a b c)")
            nc.gpsimd.memset(wa2[:], 0.0)
            nc.gpsimd.memset(wb2[:], 0.0)
            nc.gpsimd.memset(wv2[:], 0.0)
            nc.gpsimd.memset(ba_diag[:], 0.0).then_inc(s_wz, 1)
            nc.gpsimd.memset(yflat, 0.0)
            nc.gpsimd.memset(tflat, 0.0)
            nc.gpsimd.memset(ident[:], 0.0)
            nc.gpsimd.memset(nident[:], 0.0)
            nc.gpsimd.memset(avg_c[:], 1.0 / GROUP).then_inc(s_zero, 1)
            pool.wait_ge(s_zero, 1)
            nc.gpsimd.affine_select(out=yflat[:, 0:TAPS * UP].rearrange("p (k u) -> p k u", k=TAPS),
                                    in_=yflat[:, 0:TAPS * UP].rearrange("p (k u) -> p k u", k=TAPS),
                                    compare_op=ALU.not_equal, fill=1.0, base=0,
                                    pattern=[[1, TAPS], [-1, UP]], channel_multiplier=2)
            nc.gpsimd.affine_select(out=tflat[:, 0:TAPS * DB].rearrange("p (k u) -> p k u", k=TAPS),
                                    in_=tflat[:, 0:TAPS * DB].rearrange("p (k u) -> p k u", k=TAPS),
                                    compare_op=ALU.not_equal, fill=1.0, base=-1,
                                    pattern=[[1, TAPS], [-2, DB]], channel_multiplier=1)
            mr = tflat[0:RR, TAPS * DB:TAPS * (DB + IMG * DR)].rearrange("p (k i q) -> p k i q", k=TAPS, i=IMG)
            o = TAPS * (DB + IMG * DR)
            mo = tflat[0:RR, o:o + IMG * REM].rearrange("p (i q) -> p i q", i=IMG)
            nc.gpsimd.affine_select(out=mr, in_=mr, compare_op=ALU.not_equal, fill=1.0, base=-IMG,
                                    pattern=[[IMG, TAPS], [-1, IMG], [-2 * IMG, DR]], channel_multiplier=1)
            nc.gpsimd.affine_select(out=mo, in_=mo, compare_op=ALU.not_equal, fill=1.0, base=0,
                                    pattern=[[-1, IMG], [-IMG, REM]], channel_multiplier=1)
            nc.gpsimd.affine_select(out=ident[:], in_=ident[:], compare_op=ALU.not_equal, fill=1.0, base=0,
                                    pattern=[[-1, P]], channel_multiplier=1)
            nc.gpsimd.affine_select(out=nident[:], in_=nident[:], compare_op=ALU.not_equal, fill=-1.0, base=0,
                                    pattern=[[-1, P]], channel_multiplier=1).then_inc(s_zero, 1)
            pool.wait_ge(s_zero, 2)
            a3 = avg_c[:].rearrange("p (g c) -> p g c", c=GROUP)
            nc.gpsimd.affine_select(out=a3, in_=a3, compare_op=ALU.is_ge, fill=0.0, base=0,
                                    pattern=[[-GROUP, NG], [0, GROUP]], channel_multiplier=1).then_inc(s_zero, 1)
            pool.wait_ge(s_zero, 3)
            nc.gpsimd.affine_select(out=a3, in_=a3, compare_op=ALU.is_ge, fill=0.0, base=GROUP - 1,
                                    pattern=[[GROUP, NG], [0, GROUP]], channel_multiplier=-1).then_inc(s_mask, 1)

            def spread(k, par):
                wait_alone(pool, s_t, k + 1)
                nc.gpsimd.tensor_copy(tspr[par][:], tmax[par][:].unsqueeze(3).to_broadcast([P, WB, HPU, HEAD])).then_inc(s_ts, 1)

            with pool.Fori(0, UNITS * NBLK // 2) as k:
                spread(2 * k, 0)
                spread(2 * k + 1, 1)

        @block.scalar
        def _(act):
            act.sem_inc(s_y, YCREDIT)
            for started in (s_al, s_z1, s_zr):
                act.sem_inc(started, ONE)

            def unit(u):
                act.wait_ge(s_var0, u + 1)
                act.activation(t0, v0, ACT.Sqrt).then_inc(s_sq0, 1)

                def exp_b(k, par, prev, nxt):
                    bb = NBLK * u + k
                    act.wait_ge(s_nm, bb + 1)
                    act.activation(pe_[par][:, :], b_ps[par], ACT.Exp, bias=bexp[:, par:par + 1],
                                   accum_out=sblk[:, par:par + 1]).then_inc(s_p, 1)
                    act.activation(alpha[:, par:par + 1], nrun[:, 1 - par:2 - par], ACT.Exp, scale=-1.0,
                                   bias=nrun[:, par:par + 1]).then_inc(s_al, 1)
                    if prev:
                        act.wait_ge(s_pt, bb)
                        act.activation(pt_[1 - par][:, :], pt_ps[1 - par], ACT.Copy).then_inc(s_ptc, 1)

                steps(act, NBLK, exp_b)
                act.wait_ge(s_pt, NBLK * (u + 1))
                act.activation(pt_[1][:, :], pt_ps[1], ACT.Copy).then_inc(s_ptc, 1)

                def to_bf16(k, par):
                    act.activation(xb_[par][:, :, :], xc_wh[:, bass.ts(k, WB), :], ACT.Identity,
                                   bias=nm0).then_inc(s_xb, 1)

                def exp_v(k, par, prev, nxt):
                    if nxt:
                        to_bf16(k + 1, 1 - par)
                    act.wait_ge(s_v, NBLK * u + k + 1)
                    act.activation(ev_[par][:, :], v_ps[par], ACT.Exp, bias=bvs[:, 0:1]).then_inc(s_e, 1)

                to_bf16(0, 0)
                steps(act, NBLK, exp_v)

                act.wait_ge(s_var1, u + 1)
                act.activation(v1[:, :], v1[:, :], ACT.Sqrt).then_inc(s_sq1, 1)

                def batch(j, par, prev, nxt):
                    g = NBAT * u + j
                    c0 = (u % CPB) * P + j * IMG

                    def down_copy(half):
                        act.wait_ge(s_dz, 2 * g + half + 1)
                        act.activation(z1[:, half, :, :, :].rearrange("p a b c -> p a (b c)"), dz_ps,
                                       ACT.Copy).then_inc(s_z1, 1)

                    act.wait_ge(s_yrp, g + 1)
                    act.wait_ge(s_zrp, g + ONE)
                    act.activation(yr[:, :], s1_ps[0:RR, 0:UP], ACT.Identity, scale=UPGAIN * GAIN,
                                   bias=bias_r[:, bass.ds((u % CPB) * NBAT + j, 1)]).then_inc(s_yr, 1)
                    for i in range(IMG):
                        act.wait_ge(s_yp, IMG * g + i + 1)
                        act.activation(yb[:, :, :, i], y_ps[i % 2], ACT.Identity, scale=UPGAIN * GAIN,
                                       bias=bias_b[:, bass.ds(c0 + i, 1)]).then_inc(s_y, 1)
                        if i == HALF:
                            down_copy(0)
                    down_copy(1)
                    act.wait_ge(s_zrp, g + 1 + ONE)
                    act.activation(zr[:, :], s1_ps[0:RR, 0:H], ACT.Copy).then_inc(s_zr, 1)

                steps(act, NBAT, batch)

            act.wait_ge(s_cst, 1)
            with act.Fori(0, UNITS) as u:
                unit(u)

        @block.vector
        def _(dve):
            def c_stats(k):
                return nc.vector.bn_stats(stc[:, bass.ds(k, 1), :].rearrange("p a b -> p (a b)"), xc[:, bass.ts(k, 512)])

            dve.sem_inc(s_zn, ZCREDIT)
            for started in (s_ma, s_o):
                dve.sem_inc(started, ONE)
            n_par = 4 + 6 * HPU + REM
            dve.wait_ge(s_par, 16 * n_par)
            dve.wait_ge(s_mask, 1)
            yflat = yb[:, :, :, :].rearrange("p a b c -> p (a b c)")
            tflat = t1[:, :, :, :].rearrange("p a b c -> p (a b c)")
            nc.vector.memset(avg_p[:], 1.0 / P)
            nc.vector.memset(ones_row[:], 1.0)
            nc.vector.memset(gaug[:], 0.0)
            nc.vector.memset(xbart[:], 0.0)
            nc.vector.tensor_scalar(bias_b[:], bias_b[:], GAIN, None, ALU.mult)
            nc.vector.tensor_scalar(bias_r[:], bias_r[:], GAIN, None, ALU.mult)
            for w in range(WB):
                nc.vector.tensor_copy(bv_row4[:, w, :], bv_row[:, :])
            nc.vector.memset(up_t[:], 0.0)
            nc.vector.memset(dn_t[:], 0.0)
            nc.vector.memset(dn_r[:], 0.0).then_inc(s_cst_dve, 1)
            for k in range(TAPS):
                dve.wait_ge(s_cst_dve, k + 1)
                nc.vector.scalar_tensor_tensor(up_t[:], yflat[:, k * UP:(k + 1) * UP], f_up[:, k:k + 1], up_t[:],
                                               ALU.mult, ALU.add)
                nc.vector.scalar_tensor_tensor(dn_t[:], tflat[:, k * DB:(k + 1) * DB], f_dn[:, k:k + 1], dn_t[:],
                                               ALU.mult, ALU.add)
                o = TAPS * DB + k * IMG * DR
                nc.vector.scalar_tensor_tensor(dn_r[:].rearrange("p i q -> p (i q)"), tflat[0:RR, o:o + IMG * DR],
                                               f_dn[0:RR, k:k + 1], dn_r[:].rearrange("p i q -> p (i q)"),
                                               ALU.mult, ALU.add).then_inc(s_cst_dve, 1)
            for h in range(HPU):
                nc.vector.memset(gaug[h * HEAD:(h + 1) * HEAD, h, HEAD:HEAD + 1], 1.0)
            o = TAPS * (DB + IMG * DR)
            nc.vector.tensor_reduce(own[:], tflat[0:RR, o:o + IMG * REM].rearrange("p (i q) -> p i q", i=IMG), AX.X,
                                    ALU.add)
            dve.wait_ge(s_cst_dve, TAPS + 1)
            nc.vector.tensor_reduce(dn_rs[:], dn_r[:].rearrange("p i q -> p q i"), AX.X, ALU.add).then_inc(s_cst, 1)
            for i in range(XCH):
                dve.wait_ge(s_xc[i], 16)
            with dve.Fori(0, NBLK) as k:
                c_stats(k)

            def unit(u, more):
                n = [0]

                def link(ins):
                    ins.then_inc(s_small, 1)
                    n[0] += 1
                    wait_alone(dve, s_small, N_SMALL * u + n[0])

                link(nc.vector.memset(srun[:], 0.0))
                link(nc.vector.bn_aggr(mvc[:], stc[:].rearrange("p a b -> p (a b)")))
                link(nc.vector.tensor_tensor(t0, mvc[:, 0:1], mvc[:, 0:1], ALU.mult))
                nc.vector.tensor_tensor(mvc[:, 1:2], mvc[:, 1:2], t0, ALU.add).then_inc(s_gn0, 1)
                dve.wait_ge(s_gn0p, u + 1)
                link(nc.vector.tensor_copy(sc[:, 6:8], tiny[:, 0:2]))
                link(nc.vector.tensor_copy(m0, sc[:, 6:7]))
                link(nc.vector.tensor_tensor(t0, m0, m0, ALU.mult))
                link(nc.vector.tensor_tensor(v0, sc[:, 7:8], t0, ALU.subtract))
                nc.vector.tensor_scalar(v0, v0, 0.0, EPS, ALU.max, ALU.add).then_inc(s_var0, 1)
                dve.wait_ge(s_sq0, u + 1)
                link(nc.vector.reciprocal(r0, t0))
                link(nc.vector.tensor_scalar(nm0, m0, -1.0, None, ALU.mult))
                link(nc.vector.tensor_tensor(nmr0, nm0, r0, ALU.mult))
                link(nc.vector.tensor_scalar(wvs[:], wv2[:], r0, None, ALU.mult))
                link(nc.vector.tensor_scalar(wbs[:], wb2[:], r0, None, ALU.mult))
                nc.vector.tensor_copy(wvh[:], wvs[:])
                nc.vector.memset(nrun[:, 1:2], BIG)
                nc.vector.memset(mrun[:], 0.0).then_inc(s_w, 1)
                dve.wait_ge(s_bvp, u + 1)
                link(nc.vector.tensor_tensor(bvs[:], tiny[:, 4:5], bv_col[:], ALU.add))
                link(nc.vector.tensor_tensor(bbs[:], tiny[:, 5:6], bb_col[:], ALU.add))

                def add_block(bb, par):
                    dve.wait_ge(s_m, bb + 1)
                    dve.wait_ge(s_al, bb + 1 + ONE)
                    nc.vector.scalar_tensor_tensor(srun[:], srun[:], alpha[:, par:par + 1], sblk[:, par:par + 1],
                                                   ALU.mult, ALU.add)
                    nc.vector.scalar_tensor_tensor(mrun[:], mrun[:], alpha[:, par:par + 1], m_ps,
                                                   ALU.mult, ALU.add).then_inc(s_ma, 1)

                def max_b(k, par, prev, nxt):
                    bb = NBLK * u + k
                    dve.wait_ge(s_b, bb + 1)
                    nc.vector.tensor_reduce(nblk[:, par:par + 1], b_ps[par], AX.X, ALU.max,
                                            negate=True).then_inc(s_nblk, 1)
                    dve.wait_ge(s_nblk, 2 * bb + 1)
                    dve.wait_ge(s_al, bb + ONE)
                    nc.vector.scalar_tensor_tensor(nrun[:, par:par + 1], nblk[:, par:par + 1], bbs[:, 0:1],
                                                   nrun[:, 1 - par:2 - par], ALU.subtract, ALU.min).then_inc(s_nblk, 1)
                    dve.wait_ge(s_nblk, 2 * bb + 2)
                    nc.vector.tensor_tensor(bexp[:, par:par + 1], nrun[:, par:par + 1], bbs[:], ALU.add).then_inc(s_nm, 1)
                    if prev:
                        dve.wait_ge(s_ma, bb - 1 + ONE)
                        add_block(bb - 1, 1 - par)
                    wait_alone(dve, s_nm, bb + 1)

                steps(dve, NBLK, max_b)
                dve.wait_ge(s_ma, NBLK * (u + 1) - 1 + ONE)
                add_block(NBLK * (u + 1) - 1, 1)
                dve.wait_ge(s_ma, NBLK * (u + 1) + ONE)

                link(nc.vector.reciprocal(rsum[:], srun[:]))
                nc.vector.tensor_scalar(xbar[:], mrun[:], rsum[:], None, ALU.mult).then_inc(s_xbar, 1)
                dve.wait_ge(s_xbp, u + 1)
                for h in range(HPU):
                    d = slice(h * HEAD, (h + 1) * HEAD)
                    last = nc.vector.tensor_scalar(xbart[d, d], tiny[d, d], r0[d, :], nmr0[d, :], ALU.mult, ALU.add)
                last.then_inc(s_xbt, 1)
                dve.wait_ge(s_gp, u + 1)
                nc.vector.tensor_tensor(gaug[:, :, 0:HEAD], tiny[:, P:2 * P].rearrange("p (h m) -> p h m", h=HPU),
                                        ba_diag[:].rearrange("p (h m) -> p h m", h=HPU), ALU.add).then_inc(s_g, 1)

                def add_z(k, par):
                    bb = NBLK * u + k
                    dve.wait_ge(s_zz, bb + 1)
                    nc.vector.reciprocal(rinv[:].rearrange("p w h -> p (w h)"),
                                         z_ps[par][:, :, HEAD:HPU * (HEAD + 1):HEAD + 1]).then_inc(s_zn, 1)
                    dve.wait_ge(s_zn, 2 * bb + 1 + ZCREDIT)
                    zv = z_ps[par][:, :, 0:HPU * (HEAD + 1)].rearrange("p w (h m) -> p w h m", h=HPU)[:, :, :, 0:HEAD]
                    nc.vector.tensor_tensor(zs_[par][:], zv, rinv[:].unsqueeze(3).to_broadcast([P, WB, HPU, HEAD]),
                                            ALU.mult).then_inc(s_zn, 1)
                    dve.wait_ge(s_zn, 2 * bb + 2 + ZCREDIT)
                    xv = xh_wc[:, bass.ts(k, WB), :]
                    nc.vector.tensor_tensor(xv, xv, zs_[par][:].rearrange("p w h m -> p w (h m)"),
                                            ALU.add).then_inc(s_x1, 1)

                def max_v(k, par, prev, nxt):
                    dve.wait_ge(s_vt, NBLK * u + k + 1)
                    nc.vector.tensor_reduce(tmax[par][:].rearrange("p w h -> p (w h)"),
                                            vt_ps[par].rearrange("p (a n) -> p a n", n=HEAD), AX.X,
                                            ALU.max).then_inc(s_t, 1)
                    if prev is None or not prev:
                        return
                    add_z_lag(k, par)

                def add_z_lag(k, par):
                    add_z(k - 2, par)

                max_v(0, 0, False, True)
                max_v(1, 1, False, True)
                with dve.Fori(1, NBLK // 2) as kk:
                    max_v(2 * kk, 0, True, True)
                    max_v(2 * kk + 1, 1, True, True)
                add_z(NBLK - 2, 0)
                add_z(NBLK - 1, 1)
                wait_alone(dve, s_x1, NBLK * (u + 1))

                for gr in range(NG):
                    for q in range(4):
                        c = gr * GROUP + q * 4
                        last = nc.vector.bn_stats(sth[:, gr, q, :], xh[:, c:c + 4, :].rearrange("p c w -> p (c w)"))
                link(last)
                for gr in range(NG):
                    last = nc.vector.bn_aggr(mvh[:, gr, :], sth[:, gr, :, :].rearrange("p a b -> p (a b)"))
                link(last)
                link(nc.vector.tensor_tensor(v1[:], mvh[:, :, 0], mvh[:, :, 0], ALU.mult))
                nc.vector.tensor_tensor(mvh[:, :, 1], mvh[:, :, 1], v1[:], ALU.add).then_inc(s_gn1, 1)
                dve.wait_ge(s_gn1p, u + 1)
                t2 = tiny[:, 0:2 * NG].rearrange("p (g t) -> p g t", t=2)
                link(nc.vector.tensor_copy(m1[:], t2[:, :, 0]))
                link(nc.vector.tensor_tensor(v1[:], m1[:], m1[:], ALU.mult))
                link(nc.vector.tensor_tensor(v1[:], t2[:, :, 1], v1[:], ALU.subtract))
                nc.vector.tensor_scalar(v1[:], v1[:], 0.0, EPS, ALU.max, ALU.add).then_inc(s_var1, 1)
                dve.wait_ge(s_sq1, u + 1)
                link(nc.vector.reciprocal(r1[:], v1[:]))

                def norm(j, par, gr):
                    nc.vector.tensor_scalar(xn[:, par, :, :], xh[:, bass.ts(j, IMG), :], m1[:, bass.ds(gr, 1)],
                                            r1[:, bass.ds(gr, 1)], ALU.subtract, ALU.mult).then_inc(s_xn, 1)

                def copy_t1(g, i, par):
                    dve.wait_ge(s_s1, IMG * g + i + 1)
                    nc.vector.tensor_copy(t1[:, par, :, i], s1_ps[:, 0:UP]).then_inc(s_t1, 1)

                def add_out(g, j, half):
                    dve.wait_ge(s_op, 2 * g + half + 1)
                    v = xh[:, bass.ds(j * IMG + half * HALF, HALF), :].rearrange("p c w -> p (c w)")
                    nc.vector.tensor_tensor(v, o_ps, v, ALU.add).then_inc(s_o, 1)

                norm(0, 0, 0)
                norm(1, 1, 0)
                for i in range(IMG):
                    copy_t1(NBAT * u, i, 0)

                def batch(j, par, prev, nxt):
                    g = NBAT * u + j
                    if more:
                        if isinstance(j, int) and j == 0:
                            for i in range(XCH):
                                pass
                    for i in range(IMG):
                        if i == 0:
                            dve.wait_ge(s_yr, g + 1)
                            nc.vector.scalar_tensor_tensor(yr[:], yr[:], SLOPE, yr[:], ALU.mult,
                                                           ALU.max).then_inc(s_yrc, 1)
                            dve.wait_ge(s_yrc, 3 * g + 1)
                            nc.vector.tensor_scalar(yr[:], yr[:], CLAMP, -CLAMP, ALU.min, ALU.max).then_inc(s_yrc, 1)
                            dve.wait_ge(s_yrc, 3 * g + 2)
                            nc.vector.tensor_tensor(yrb[:], yr[:, 2 * P:UP].unsqueeze(2).to_broadcast([RR, REM, IMG]),
                                                    own[:].unsqueeze(1).to_broadcast([RR, REM, IMG]), ALU.mult).then_inc(s_yrc, 1)
                        dve.wait_ge(s_y, IMG * g + i + 1 + YCREDIT)
                        nc.vector.scalar_tensor_tensor(yb[:, :, :, i], yb[:, :, :, i], SLOPE, yb[:, :, :, i], ALU.mult,
                                                       ALU.max).then_inc(s_lr, 1)
                        if nxt:
                            copy_t1(g + 1, i, 1 - par)
                        dve.wait_ge(s_lr, IMG * g + i + 1)
                        nc.vector.tensor_scalar(yb[:, :, :, i], yb[:, :, :, i], CLAMP, -CLAMP, ALU.min,
                                                ALU.max).then_inc(s_yc, 1)
                        if prev and i in (2, 4):
                            add_out(g - 1, j - 1, i // 4)
                        if more and i in (3, 6):
                            for q in range(XCH):
                                pass
                            c_stats(2 * j + i // 6)

                def batch_and_norm(j, par, prev, nxt):
                    batch(j, par, prev, nxt)
                    if two_on(j):
                        norm(j + 2, par, (j + 2) // 2 if isinstance(j, int) else j // 2 + 1)

                def two_on(j):
                    return not isinstance(j, int) or j + 2 < NBAT

                if more:
                    for q in range(XCH):
                        wait_alone(dve, s_xc[q], 16 * (u + 2))
                batch_and_norm(0, 0, False, True)
                batch_and_norm(1, 1, True, True)
                with dve.Fori(1, NBAT // 2 - 1) as k:
                    batch(2 * k, 0, True, True)
                    norm(2 * k + 2, 0, k + 1)
                    batch(2 * k + 1, 1, True, True)
                    norm(2 * k + 3, 1, k + 1)
                batch(NBAT - 2, 0, True, True)
                batch(NBAT - 1, 1, True, False)
                for half in range(2):
                    add_out(NBAT * (u + 1) - 1, NBAT - 1, half)
                assert n[0] == N_SMALL, n[0]

            with dve.Fori(0, UNITS - 1) as u:
                unit(u, True)
            unit(UNITS - 1, False)

        @block.tensor
        def _(pe):
            def mm(o, l, r, start, stop=True, share=False):
                return nc.tensor.matmul(o, l, r, start=start, stop=stop, skip_group_check=share)

            pe.sem_inc(s_zrp, ONE)

            def unit(u):
                pe.wait_ge(s_gn0, u + 1)
                pe.wait_ge(s_z1, 2 * NBAT * u + ONE)
                mm(tiny[:, 0:2], avg_c[:], mvc[:], True).then_inc(s_gn0p, 1)
                pe.wait_ge(s_w, u + 1)
                mm(tiny[:, 5:6], wbs[:], nm0, True)
                mm(tiny[:, 4:5], wvs[:], nm0, True).then_inc(s_bvp, 1)

                def proj_b(k, par):
                    mm(b_ps[par], wbs[:], xc_wh[:, bass.ts(k, WB), :], True).then_inc(s_b, 1)

                def sum_block(bb, k, par):
                    pe.wait_ge(s_ptc, bb + 1)
                    pe.wait_ge(s_ma, bb + ONE)
                    for w in range(WB):
                        last = mm(m_ps, pt_[par][:, w * H:(w + 1) * H], xh_wc[:, WB * k + w, :], w == 0, w == WB - 1)
                    last.then_inc(s_m, 1)

                def attend(k, par, prev, nxt):
                    bb = NBLK * u + k
                    if nxt:
                        proj_b(k + 1, 1 - par)
                    pe.wait_ge(s_p, bb + 1)
                    for w in range(WB):
                        last = nc.tensor.transpose(pt_ps[par][:, w * H:(w + 1) * H], pe_[par][:, w * H:(w + 1) * H],
                                                   ident[:])
                    last.then_inc(s_pt, 1)
                    if prev:
                        sum_block(bb - 1, k - 1, 1 - par)

                pe.wait_ge(s_y, IMG * NBAT * u + YCREDIT)
                proj_b(0, 0)
                for i in range(2):
                    pe.wait_ge(s_xh[i], 16 * NBAT // 2 * (u + 1))
                steps(pe, NBLK, attend)
                sum_block(NBLK * (u + 1) - 1, NBLK - 1, 1)

                pe.wait_ge(s_xbar, u + 1)
                nc.tensor.transpose(tiny[:, 0:P], xbar[:], ident[:]).then_inc(s_xbp, 1)
                pe.wait_ge(s_xbt, u + 1)
                mm(tiny[:, P:2 * P], xbart[:], wa2[:], True).then_inc(s_gp, 1)

                def v_t(k, par):
                    pe.wait_ge(s_xb, NBLK * u + k + 1)
                    mm(vt_ps[par], ones_row[:], bv_row4[:].rearrange("a w n -> a (w n)"), True)
                    for w in range(WB):
                        last = mm(vt_ps[par][:, w * P:(w + 1) * P], xb_[par][:, w, :], wvh[:], False, True,
                                  share=True)
                    last.then_inc(s_vt, 1)

                def z(k, par):
                    pe.wait_ge(s_e, NBLK * u + k + 1)
                    pe.wait_ge(s_zn, 2 * (NBLK * u + k - 2) + 2 + ZCREDIT)
                    for w in range(WB):
                        last = mm(z_ps[par][:, w, 0:HPU * (HEAD + 1)], ev_[par][:, w * H:(w + 1) * H],
                                  gaug[:].rearrange("p h m -> p (h m)"), True)
                    last.then_inc(s_zz, 1)

                def values(k, par, prev, nxt):
                    mm(v_ps[par], wvs[:], xc_wh[:, bass.ts(k, WB), :], True)
                    if prev:
                        z(k - 1, 1 - par)
                    pe.wait_ge(s_ts, NBLK * u + k + 1)
                    for w in range(WB):
                        last = mm(v_ps[par][:, w * H:(w + 1) * H],
                                  tspr[par][:, w, :, :].rearrange("p h m -> p (h m)"), nident[:], False,
                                  True, share=True)
                    last.then_inc(s_v, 1)
                    if nxt:
                        v_t(k + 1, 1 - par)

                v_t(0, 0)
                pe.wait_ge(s_g, u + 1)
                steps(pe, NBLK, values)
                z(NBLK - 1, 1)

                pe.wait_ge(s_gn1, u + 1)
                mm(tiny[:, 0:2 * NG], avg_p[:], mvh[:].rearrange("p g t -> p (g t)"), True).then_inc(s_gn1p, 1)

                def up_rows(g, i, par):
                    if i == 0:
                        pe.wait_ge(s_xn, g + 1)
                    else:
                        pe.wait_ge(s_t1, IMG * g + i)
                    mm(s1_ps[:, 0:UP], xn[:, par, i, :], up_t[:], True).then_inc(s_s1, 1)

                def up_columns(g, i, par):
                    pe.wait_ge(s_y, IMG * g + i - 1 + YCREDIT)
                    for c in range(2):
                        last = mm(y_ps[i % 2][:, c, :], t1[:, par, c * P:(c + 1) * P, i], up_t[:], True)
                    last.then_inc(s_yp, 1)

                def down(o, la, lb, first):
                    mm(o[:, 0:DA], la, dn_t[:, DB - DA:DB], first, True, share=True)
                    return mm(o[:, DB0:H], lb, dn_t[:], False, True, share=True)

                def down_rows(g, i):
                    pe.wait_ge(s_yc, IMG * g + i + 1)
                    if i % HALF == 0:
                        pe.wait_ge(s_z1, 2 * g + i // HALF + ONE)
                    r = i % HALF
                    for c in range(2):
                        v = slice(c * P, (c + 1) * P)
                        down(dz_ps[:, c, r * H:(r + 1) * H], yb[:, 0, v, i], yb[:, 1, v, i], r == 0)
                    if r == HALF - 1:
                        half = i // HALF
                        pe.wait_ge(s_yrc, 3 * g + 3)
                        for c in range(2):
                            o = dz_ps[:, c, :].rearrange("p (r h) -> p r h", h=H)[:, :, H - DR:H]
                            last = mm(o, yr[:, c * P:(c + 1) * P], dn_r[:, half * HALF:(half + 1) * HALF, :], False,
                                      True, share=True)
                        last.then_inc(s_dz, 1)

                def down_columns(g, half):
                    pe.wait_ge(s_z1, 2 * g + half + 1 + ONE)
                    pe.wait_ge(s_zr, g + 1 + ONE)
                    pe.wait_ge(s_o, 2 * g + half + ONE)
                    for r in range(HALF):
                        down(o_ps[:, r * W:(r + 1) * W], z1[:, half, 0, r, :], z1[:, half, 1, r, :], r == 0)
                    o = o_ps.rearrange("p (r w) -> p r w", w=W)[:, :, W - DR:W]
                    mm(o, zr[:, :], dn_r[:, half * HALF:(half + 1) * HALF, :], False, True, share=True).then_inc(s_op, 1)

                def batch(j, par, prev, nxt):
                    g = NBAT * u + j
                    pe.wait_ge(s_t1, IMG * (g + 1))
                    pe.wait_ge(s_zr, g + ONE)
                    mm(s1_ps[0:RR, 0:UP], t1[:, par, 2 * P:UP, :].rearrange("p q i -> p (q i)"), up_t[:], True).then_inc(s_yrp, 1)
                    for i in range(IMG):
                        if nxt:
                            if i == 0:
                                pe.wait_ge(s_yr, g + 1)
                            up_rows(g + 1, i, 1 - par)
                        up_columns(g, i, par)
                        if i:
                            down_rows(g, i - 1)
                        if prev and i in (1, 3):
                            down_columns(g - 1, i // 2)
                    down_rows(g, IMG - 1)
                    if nxt:
                        pe.wait_ge(s_t1, IMG * (g + 2))
                    else:
                        pe.wait_ge(s_yr, g + 1)
                    down(s1_ps[0:RR, :], yb[:, 0, 2 * P:UP, :].rearrange("p q i -> p (q i)"),
                         yb[:, 1, 2 * P:UP, :].rearrange("p q i -> p (q i)"), True)
                    mm(s1_ps[0:RR, H - DR:H], yrb[:].rearrange("p q i -> p (q i)"), dn_rs[:], False, True,
                       share=True).then_inc(s_zrp, 1)

                for i in range(IMG):
                    up_rows(NBAT * u, i, 0)
                steps(pe, NBAT, batch)
                for half in range(2):
                    down_columns(NBAT * (u + 1) - 1, half)

            pe.wait_ge(s_cst, 1)
            with pe.Fori(0, UNITS) as u:
                unit(u)


def kernel(x, L0_conv_Wa, L0_conv_ba, L0_conv_Wb, L0_conv_bb, L0_conv_Wv, L0_conv_bv, L1_conv_bias, L1_conv_up_filter,
           L1_conv_down_filter):
    import numpy as np
    import concourse.bacc as bacc
    from concourse.bass_utils import run_bass_kernel_spmd

    nc = bacc.Bacc("TRN2", target_bir_lowering=False, num_devices=1)
    host = {"x": x, "WaT": np.asarray(L0_conv_Wa).T, "ba": L0_conv_ba, "WbT": np.asarray(L0_conv_Wb).T,
            "bb": L0_conv_bb, "WvT": np.asarray(L0_conv_Wv).T, "bv": L0_conv_bv, "bias": L1_conv_bias, "fup": L1_conv_up_filter,
            "fdn": L1_conv_down_filter}
    arrays, args = {}, []
    for name, a in host.items():
        a = np.ascontiguousarray(a)
        arrays["in_" + name] = a
        args.append(nc.dram_tensor("in_" + name, a.shape, mybir.dt.from_np(a.dtype), kind="ExternalInput").ap())
    o = nc.dram_tensor("out_0", (B, C, H, W), mybir.dt.float32, kind="ExternalOutput").ap()
    attention_then_filters(nc, *args, o)
    r = run_bass_kernel_spmd(nc, [arrays], core_ids=[0])
    return r.results[0]["out_0"]
```

```python
import concourse.bass as bass
from concourse import mybir
from contextlib import ExitStack

B, C, H, W = 8, 512, 128, 128
P = 128
HEAD = 64
HPU = P // HEAD
UNITS = B * C // P
CPB = C // P
GROUP = C // 32
NG = P // GROUP
EPS = 1e-5
WB = 4
NBLK = W // WB
BS = WB * H
RING = 4
XCH = 4
IMG = 8
NBAT = P // IMG
YRING = 4
LAG = 2
HALF = IMG // 2
TAPS = 12
UP = 2 * H + 10
REM = UP - 2 * P
RR = IMG * REM
DA, DB = 64, 69
DB0 = H - DB
DR = 5
SLOPE, CLAMP = 0.2, 256.0
GAIN = 2.0 ** 0.5
UPGAIN = 4.0
BIG = 3.0e38
N_SMALL = 22


def attention_then_filters(nc, x, WaT, ba, WbT, bb_, WvT, bv, bias, fup, fdn, out):
    fp32, bf16 = mybir.dt.float32, mybir.dt.bfloat16
    ALU, ACT, AX = mybir.AluOpType, mybir.ActivationFunctionType, mybir.AxisListType

    x_ch = x.rearrange("b (u c) h w -> (b u) c (h w)", c=P)
    x_row = x.rearrange("b (u c) h w -> (b u) h c w", c=P)
    out_row = out.rearrange("b (u c) h w -> (b u) h c w", c=P)

    ctx = ExitStack()
    with ctx:
        def sb(name, shape, dt=fp32):
            return ctx.enter_context(nc.sbuf_tensor(name, shape, dt))

        def pb(name, shape, dt=fp32):
            return ctx.enter_context(nc.psum_tensor(name, shape, dt))

        def sem(name):
            return ctx.enter_context(nc.semaphore(name))

        xc = sb("xc", [P, H * W])
        xh = sb("xh", [P, P, W])
        xc_wh = xc[:, :].rearrange("c (h w) -> c w h", w=W)
        xh_wc = xh[:, :, :].rearrange("h c w -> h w c")
        ident = sb("ident", [P, P])
        nident = sb("nident", [P, P], bf16)
        avg_c = sb("avg_c", [P, P])
        avg_p = sb("avg_p", [P, P])
        wa2 = sb("wa2", [P, P])
        wb2 = sb("wb2", [P, P])
        wv2 = sb("wv2", [P, P])
        ba_diag = sb("ba_diag", [P, P])
        bb_col = sb("bb_col", [P, 1])
        bv_col = sb("bv_col", [P, 1])
        bv_row = sb("bv_row", [1, P])
        bv_row4 = sb("bv_row4", [1, WB, P], bf16)
        ones_row = sb("ones_row", [1, P], bf16)
        up_t = sb("up_t", [P, UP])
        dn_t = sb("dn_t", [P, DB])
        dn_r = sb("dn_r", [RR, IMG, DR])
        dn_rs = sb("dn_rs", [RR, DR])
        own = sb("own", [RR, IMG])
        f_up = sb("f_up", [P, TAPS])
        f_dn = sb("f_dn", [P, TAPS])
        bias_b = sb("bias_b", [P, C])
        bias_r = sb("bias_r", [RR, C // IMG])
        wbs = sb("wbs", [P, P])
        wvs = sb("wvs", [P, P])
        wvh = sb("wvh", [P, P], bf16)
        bvs = sb("bvs", [P, 1])
        bbs = sb("bbs", [P, 1])
        stc = sb("stc", [P, NBLK, 6])
        mvc = sb("mvc", [P, 2])
        sc = sb("sc", [P, 12])
        m0, nm0, r0, nmr0, v0, t0 = (sc[:, i:i + 1] for i in range(6))
        nblk = sb("nblk", [P, 2])
        nrun = sb("nrun", [P, RING])
        bexp = sb("bexp", [P, RING])
        alpha = sb("alpha", [P, RING])
        sblk = sb("sblk", [P, RING])
        srun = sb("srun", [P, 1])
        rsum = sb("rsum", [P, 1])
        mrun = sb("mrun", [P, P])
        xbar = sb("xbar", [P, P])
        xbart = sb("xbart", [P, P])
        gaug = sb("gaug", [P, HPU, HEAD + 1])
        pe_ = [sb(f"p{i}", [P, BS]) for i in range(2)]
        pt_ = [sb(f"pt{i}", [P, BS]) for i in range(2)]
        xb_ = [sb(f"xb{i}", [P, WB, P], bf16) for i in range(2)]
        ev_ = pe_
        tmax = [sb(f"tmax{i}", [P, WB, HPU], bf16) for i in range(2)]
        tspr = [sb(f"tspr{i}", [P, WB, HPU, HEAD], bf16) for i in range(2)]
        rinv = sb("rinv", [P, WB, HPU])
        zs_ = [t[:, :].rearrange("p (w h m) -> p w h m", w=WB, h=HPU) for t in pt_]
        sth = sb("sth", [P, NG, 4, 6])
        mvh = sb("mvh", [P, NG, 2])
        m1 = sb("m1", [P, NG])
        r1 = sb("r1", [P, NG])
        v1 = sb("v1", [P, NG])
        xn = sb("xn", [P, 2, IMG, W])
        t1 = sb("t1", [P, 2, UP, IMG])
        yb = sb("yb", [P, YRING, 2, UP])
        yc = sb("yc", [P, 2, 2, REM, IMG])
        yr = sb("yr", [RR, 2, UP])
        yrb = sb("yrb", [RR, 2, REM, IMG])
        z1 = sb("z1", [P, 2, 2, HALF, H])
        zr = sb("zr", [RR, H])

        ps = pb("ps", [P, 8, 512])
        b_ps = [ps[:, i, :] for i in (0, 1, 6, 7)]
        pt_ps = [ps[:, i, :] for i in (2, 3)]
        m_ps = ps[:, 4, 0:P]
        tiny = ps[:, 5, :]
        v_ps = b_ps[0:2]
        z_ps = [ps[:, i:i + 2, :].rearrange("p b (w n) -> p (b w) n", w=2) for i in (2, 4)]
        vt_ps = [ps[:, i, :] for i in (6, 7)]
        y_ps = [ps[:, i:i + 2, 0:UP] for i in (0, 2)]
        dz_ps = ps[:, 4:6, :]
        s1_ps = ps[:, 6, :]
        o_ps = ps[:, 7, :]

        s_par = sem("parameters_loaded")
        s_zero = sem("zeros_set")
        s_mask = sem("masks_set")
        s_wz = sem("weights_zeroed")
        s_cst_dve = sem("constant_steps")
        s_cst = sem("constants_ready")
        s_xc = [sem(f"xc_piece{i}_loaded") for i in range(XCH)]
        s_xh = [sem(f"xh_loaded_{i}") for i in range(2)]
        s_st = [sem(f"out_stored_{i}") for i in range(2)]
        s_small = sem("vector_small_steps")
        s_gn0 = sem("norm0_stats_ready")
        s_gn0p = sem("norm0_averaged")
        s_var0 = sem("norm0_variance_ready")
        s_sq0 = sem("norm0_sqrt_ready")
        s_w = sem("scaled_weights_ready")
        s_bvp = sem("value_bias_product")
        s_b = sem("b_scores_in_psum")
        s_nblk = sem("block_max_ready")
        s_nm = sem("running_max_ready")
        s_p = sem("exp_b_ready")
        s_al = sem("alpha_ready")
        s_pt = sem("exp_b_transposed")
        s_ptc = sem("exp_b_transposed_copied")
        s_m = sem("block_sum_in_psum")
        s_ma = sem("block_sum_added")
        s_xbar = sem("xbar_ready")
        s_xbp = sem("xbar_transposed")
        s_xbt = sem("xbar_t_ready")
        s_gp = sem("g_in_psum")
        s_g = sem("g_ready")
        s_xb = sem("xc_bf16_ready")
        s_vt = sem("v_transposed_in_psum")
        s_t = sem("v_max_ready")
        s_ts = sem("v_max_spread")
        s_v = sem("v_in_psum")
        s_e = sem("exp_v_ready")
        s_zz = sem("z_in_psum")
        s_zn = sem("z_normalised")
        s_x1 = sem("x1_written")
        s_gn1 = sem("norm1_stats_ready")
        s_gn1p = sem("norm1_averaged")
        s_var1 = sem("norm1_variance_ready")
        s_sq1 = sem("norm1_sqrt_ready")
        s_xn = sem("xn_ready")
        s_s1 = sem("up_rows_in_psum")
        s_t1 = sem("up_rows_copied")
        s_yp = sem("up_2d_in_psum")
        s_y = sem("up_2d_scaled")
        s_lr = sem("leaky_relu_done")
        s_yc = sem("clipped")
        s_yrp = sem("remainder_rows_in_psum")
        s_yr = sem("remainder_rows_scaled")
        s_yrc = sem("remainder_rows_clipped")
        s_dz = sem("down_rows_in_psum")
        s_z1 = sem("down_rows_copied")
        s_zrp = sem("remainder_columns_in_psum")
        s_zr = sem("remainder_columns_copied")
        s_op = sem("output_in_psum")
        s_o = sem("output_added")

        ZCREDIT = 4
        s_alone = sem("lone_waits")

        ACREDIT = 3
        ONE = 1
        YCREDIT = 2

        block = ctx.enter_context(nc.Block())

        def wait_alone(eng, semaphore, value):
            eng.wait_ge(semaphore, value)
            eng.sem_inc(s_alone, 1)

        def steps(eng, n, unroll, step):
            for r in range(unroll):
                step(r, r, lambda b: r >= b, lambda a: True)
            with eng.Fori(1, n // unroll - 1) as k:
                for r in range(unroll):
                    step(unroll * k + r, r, lambda b: True, lambda a: True)
            for r in range(unroll):
                step(n - unroll + r, r, lambda b: True, lambda a: r + a < unroll)

        @block.sync
        def _(sp):
            def load_xc(u):
                n = H * W // XCH
                for i in range(XCH):
                    sp.dma_start(xc[:, i * n:(i + 1) * n], x_ch[u, :, i * n:(i + 1) * n]).then_inc(s_xc[i], 16)

            def load_xh(u, j, par):
                sp.dma_start(xh[:, bass.ts(j, IMG), :], x_row[u, :, bass.ts(j, IMG), :]).then_inc(s_xh[par], 16)

            load_xc(0)
            sp.dma_start(f_up[:, :], fup.rearrange("(a n) -> a n", a=1).to_broadcast([P, TAPS])).then_inc(s_par, 16)
            sp.dma_start(f_dn[:, :], fdn.rearrange("(a n) -> a n", a=1).to_broadcast([P, TAPS])).then_inc(s_par, 16)
            sp.dma_start(bias_b[:, :], bias.rearrange("(a n) -> a n", a=1).to_broadcast([P, C])).then_inc(s_par, 16)
            sp.dma_start(bv_row[:, :].rearrange("a (t n) -> a t n", t=HPU),
                         bv.rearrange("(a t n) -> a t n", a=1, t=1).to_broadcast([1, HPU, HEAD])).then_inc(s_par, 16)
            sp.wait_ge(s_wz, 1)
            for h in range(HPU):
                d = slice(h * HEAD, (h + 1) * HEAD)
                for dst, src in ((wa2, WaT), (wb2, WbT), (wv2, WvT)):
                    sp.dma_start(dst[d, d], src).then_inc(s_par, 16)
                sp.dma_start(ba_diag[d, d], ba.rearrange("(a n) -> a n", a=1).to_broadcast([HEAD, HEAD])).then_inc(s_par, 16)
                sp.dma_start(bb_col[d, :], bb_.rearrange("(n a) -> n a", a=1)).then_inc(s_par, 16)
                sp.dma_start(bv_col[d, :], bv.rearrange("(n a) -> n a", a=1)).then_inc(s_par, 16)
            for i in range(REM):
                sp.dma_start(bias_r[i * IMG:(i + 1) * IMG, :], bias.rearrange("(t n) -> n t", n=IMG),
                             allow_slow_non_contiguous=True).then_inc(s_par, 16)
            sp.wait_ge(s_cst, 1)
            for j in range(NBAT):
                load_xh(0, j, j % 2)

            def unit(u, more):
                if more:
                    wait_alone(sp, s_v, NBLK * (u + 1))
                    wait_alone(sp, s_xb, NBLK * (u + 1))
                    load_xc(u + 1)

                def batch(j, par, before, after):
                    wait_alone(sp, s_o, 2 * (NBAT * u + j + 1) + ONE)
                    sp.dma_start(out_row[u, :, bass.ts(j, IMG), :], xh[:, bass.ts(j, IMG), :]).then_inc(s_st[par], 16)
                    if before(1):
                        wait_alone(sp, s_st[1 - par], 16 * (NBAT // 2 * u + (j - 1) // 2 + 1))
                        if more:
                            load_xh(u + 1, j - 1, 1 - par)

                steps(sp, NBAT, 2, batch)
                wait_alone(sp, s_st[1], 16 * (NBAT // 2 * (u + 1)))
                if more:
                    load_xh(u + 1, NBAT - 1, 1)

            with sp.Fori(0, UNITS - 1) as u:
                unit(u, True)
            unit(UNITS - 1, False)

        @block.gpsimd
        def _(pool):
            yflat = xh[:, 0:TAPS * UP // W + 1, :].rearrange("p a b -> p (a b)")
            tflat = t1[:, :, :, :].rearrange("p a b c -> p (a b c)")
            nc.gpsimd.memset(wa2[:], 0.0)
            nc.gpsimd.memset(wb2[:], 0.0)
            nc.gpsimd.memset(wv2[:], 0.0)
            nc.gpsimd.memset(ba_diag[:], 0.0).then_inc(s_wz, 1)
            nc.gpsimd.memset(yflat, 0.0)
            nc.gpsimd.memset(tflat, 0.0)
            nc.gpsimd.memset(ident[:], 0.0)
            nc.gpsimd.memset(nident[:], 0.0)
            nc.gpsimd.memset(avg_c[:], 1.0 / GROUP).then_inc(s_zero, 1)
            pool.wait_ge(s_zero, 1)
            nc.gpsimd.affine_select(out=yflat[:, 0:TAPS * UP].rearrange("p (k u) -> p k u", k=TAPS),
                                    in_=yflat[:, 0:TAPS * UP].rearrange("p (k u) -> p k u", k=TAPS),
                                    compare_op=ALU.not_equal, fill=1.0, base=0,
                                    pattern=[[1, TAPS], [-1, UP]], channel_multiplier=2)
            nc.gpsimd.affine_select(out=tflat[:, 0:TAPS * DB].rearrange("p (k u) -> p k u", k=TAPS),
                                    in_=tflat[:, 0:TAPS * DB].rearrange("p (k u) -> p k u", k=TAPS),
                                    compare_op=ALU.not_equal, fill=1.0, base=-1,
                                    pattern=[[1, TAPS], [-2, DB]], channel_multiplier=1)
            mr = tflat[0:RR, TAPS * DB:TAPS * (DB + IMG * DR)].rearrange("p (k i q) -> p k i q", k=TAPS, i=IMG)
            o = TAPS * (DB + IMG * DR)
            mo = tflat[0:RR, o:o + IMG * REM].rearrange("p (i q) -> p i q", i=IMG)
            nc.gpsimd.affine_select(out=mr, in_=mr, compare_op=ALU.not_equal, fill=1.0, base=-IMG,
                                    pattern=[[IMG, TAPS], [-1, IMG], [-2 * IMG, DR]], channel_multiplier=1)
            nc.gpsimd.affine_select(out=mo, in_=mo, compare_op=ALU.not_equal, fill=1.0, base=0,
                                    pattern=[[-1, IMG], [-IMG, REM]], channel_multiplier=1)
            nc.gpsimd.affine_select(out=ident[:], in_=ident[:], compare_op=ALU.not_equal, fill=1.0, base=0,
                                    pattern=[[-1, P]], channel_multiplier=1)
            nc.gpsimd.affine_select(out=nident[:], in_=nident[:], compare_op=ALU.not_equal, fill=-1.0, base=0,
                                    pattern=[[-1, P]], channel_multiplier=1).then_inc(s_zero, 1)
            pool.wait_ge(s_zero, 2)
            a3 = avg_c[:].rearrange("p (g c) -> p g c", c=GROUP)
            nc.gpsimd.affine_select(out=a3, in_=a3, compare_op=ALU.is_ge, fill=0.0, base=0,
                                    pattern=[[-GROUP, NG], [0, GROUP]], channel_multiplier=1).then_inc(s_zero, 1)
            pool.wait_ge(s_zero, 3)
            nc.gpsimd.affine_select(out=a3, in_=a3, compare_op=ALU.is_ge, fill=0.0, base=GROUP - 1,
                                    pattern=[[GROUP, NG], [0, GROUP]], channel_multiplier=-1).then_inc(s_mask, 1)

            def spread(k, par):
                wait_alone(pool, s_t, k + 1)
                nc.gpsimd.tensor_copy(tspr[par][:], tmax[par][:].unsqueeze(3).to_broadcast([P, WB, HPU, HEAD])).then_inc(s_ts, 1)

            with pool.Fori(0, UNITS * NBLK // 2) as k:
                spread(2 * k, 0)
                spread(2 * k + 1, 1)

        @block.scalar
        def _(act):
            act.sem_inc(s_y, YCREDIT)
            act.sem_inc(s_al, ACREDIT)
            for started in (s_z1, s_zr):
                act.sem_inc(started, ONE)

            def unit(u):
                act.wait_ge(s_var0, u + 1)
                act.activation(t0, v0, ACT.Sqrt).then_inc(s_sq0, 1)

                def exp_b(k, r, before, after):
                    now, last = slice(r, r + 1), slice((r - 1) % RING, (r - 1) % RING + 1)
                    act.wait_ge(s_nm, NBLK * u + k + 1)
                    act.activation(alpha[:, now], nrun[:, last], ACT.Exp, scale=-1.0,
                                   bias=nrun[:, now]).then_inc(s_al, 1)
                    act.activation(pe_[r % 2][:, :], b_ps[r], ACT.Exp, bias=bexp[:, now],
                                   accum_out=sblk[:, now]).then_inc(s_p, 1)
                    if before(1):
                        act.wait_ge(s_pt, NBLK * u + k)
                        act.activation(pt_[1 - r % 2][:, :], pt_ps[1 - r % 2], ACT.Copy).then_inc(s_ptc, 1)

                steps(act, NBLK, RING, exp_b)
                act.wait_ge(s_pt, NBLK * (u + 1))
                act.activation(pt_[1][:, :], pt_ps[1], ACT.Copy).then_inc(s_ptc, 1)

                def to_bf16(k, par):
                    act.activation(xb_[par][:, :, :], xc_wh[:, bass.ts(k, WB), :], ACT.Identity,
                                   bias=nm0).then_inc(s_xb, 1)

                def exp_v(k, r, before, after):
                    par = r % 2
                    if after(2):
                        act.wait_ge(s_vt, NBLK * u + k + 1)
                        to_bf16(k + 2, par)
                    act.wait_ge(s_v, NBLK * u + k + 1)
                    act.activation(ev_[par][:, :], v_ps[par], ACT.Exp, bias=bvs[:, 0:1]).then_inc(s_e, 1)

                to_bf16(0, 0)
                to_bf16(1, 1)
                steps(act, NBLK, RING, exp_v)

                act.wait_ge(s_var1, u + 1)
                act.activation(v1[:, :], v1[:, :], ACT.Sqrt).then_inc(s_sq1, 1)

                def copy_t1(g, i, par):
                    act.wait_ge(s_s1, IMG * g + i + 1)
                    act.activation(t1[:, par, :, i], s1_ps[:, 0:UP], ACT.Copy).then_inc(s_t1, 1)

                def down_copy(g, half):
                    act.wait_ge(s_dz, 2 * g + half + 1)
                    act.activation(z1[:, half, :, :, :].rearrange("p a b c -> p a (b c)"), dz_ps,
                                   ACT.Copy).then_inc(s_z1, 1)

                def remainder_copy(g):
                    act.wait_ge(s_zrp, g + 1 + ONE)
                    act.activation(zr[:, :], s1_ps[0:RR, 0:H], ACT.Copy).then_inc(s_zr, 1)

                def batch(j, par, before, after):
                    g = NBAT * u + j
                    c0 = (u % CPB) * P + j * IMG
                    for i in range(IMG):
                        act.wait_ge(s_yp, IMG * g + i + 1)
                        act.activation(yb[:, i % YRING, :, :], y_ps[i % 2], ACT.Identity, scale=UPGAIN * GAIN,
                                       bias=bias_b[:, bass.ds(c0 + i, 1)]).then_inc(s_y, 1)
                        if after(1):
                            copy_t1(g + 1, i, 1 - par)
                        if i == 0:
                            act.wait_ge(s_yrp, g + 1)
                            act.activation(yr[:, par, :], s1_ps[0:RR, 0:UP], ACT.Identity, scale=UPGAIN * GAIN,
                                           bias=bias_r[:, bass.ds((u % CPB) * NBAT + j, 1)]).then_inc(s_yr, 1)
                        if i == LAG - 1 and before(1):
                            down_copy(g - 1, 1)
                            remainder_copy(g - 1)
                        if i == HALF - 1 + LAG:
                            down_copy(g, 0)

                for i in range(IMG):
                    copy_t1(NBAT * u, i, 0)
                steps(act, NBAT, 2, batch)
                down_copy(NBAT * (u + 1) - 1, 1)
                remainder_copy(NBAT * (u + 1) - 1)

            act.wait_ge(s_cst, 1)
            with act.Fori(0, UNITS) as u:
                unit(u)

        @block.vector
        def _(dve):
            def c_stats(k):
                return nc.vector.bn_stats(stc[:, bass.ds(k, 1), :].rearrange("p a b -> p (a b)"), xc[:, bass.ts(k, 512)])

            dve.sem_inc(s_zn, ZCREDIT)
            for started in (s_ma, s_o):
                dve.sem_inc(started, ONE)
            n_par = 4 + 6 * HPU + REM
            dve.wait_ge(s_par, 16 * n_par)
            dve.wait_ge(s_mask, 1)
            yflat = xh[:, 0:TAPS * UP // W + 1, :].rearrange("p a b -> p (a b)")
            tflat = t1[:, :, :, :].rearrange("p a b c -> p (a b c)")
            nc.vector.memset(avg_p[:], 1.0 / P)
            nc.vector.memset(ones_row[:], 1.0)
            nc.vector.memset(gaug[:], 0.0)
            nc.vector.memset(xbart[:], 0.0)
            nc.vector.tensor_scalar(bias_b[:], bias_b[:], GAIN, None, ALU.mult)
            nc.vector.tensor_scalar(bias_r[:], bias_r[:], GAIN, None, ALU.mult)
            for w in range(WB):
                nc.vector.tensor_copy(bv_row4[:, w, :], bv_row[:, :])
            nc.vector.memset(up_t[:], 0.0)
            nc.vector.memset(dn_t[:], 0.0)
            nc.vector.memset(dn_r[:], 0.0).then_inc(s_cst_dve, 1)
            for k in range(TAPS):
                dve.wait_ge(s_cst_dve, k + 1)
                nc.vector.scalar_tensor_tensor(up_t[:], yflat[:, k * UP:(k + 1) * UP], f_up[:, k:k + 1], up_t[:],
                                               ALU.mult, ALU.add)
                nc.vector.scalar_tensor_tensor(dn_t[:], tflat[:, k * DB:(k + 1) * DB], f_dn[:, k:k + 1], dn_t[:],
                                               ALU.mult, ALU.add)
                o = TAPS * DB + k * IMG * DR
                nc.vector.scalar_tensor_tensor(dn_r[:].rearrange("p i q -> p (i q)"), tflat[0:RR, o:o + IMG * DR],
                                               f_dn[0:RR, k:k + 1], dn_r[:].rearrange("p i q -> p (i q)"),
                                               ALU.mult, ALU.add).then_inc(s_cst_dve, 1)
            for h in range(HPU):
                nc.vector.memset(gaug[h * HEAD:(h + 1) * HEAD, h, HEAD:HEAD + 1], 1.0)
            o = TAPS * (DB + IMG * DR)
            nc.vector.tensor_reduce(own[:], tflat[0:RR, o:o + IMG * REM].rearrange("p (i q) -> p i q", i=IMG), AX.X,
                                    ALU.add)
            dve.wait_ge(s_cst_dve, TAPS + 1)
            nc.vector.tensor_reduce(dn_rs[:], dn_r[:].rearrange("p i q -> p q i"), AX.X, ALU.add).then_inc(s_cst, 1)
            for i in range(XCH):
                dve.wait_ge(s_xc[i], 16)
            with dve.Fori(0, NBLK) as k:
                c_stats(k)

            def unit(u, more):
                n = [0]

                def link(ins):
                    ins.then_inc(s_small, 1)
                    n[0] += 1
                    wait_alone(dve, s_small, N_SMALL * u + n[0])

                link(nc.vector.memset(srun[:], 0.0))
                link(nc.vector.bn_aggr(mvc[:], stc[:].rearrange("p a b -> p (a b)")))
                link(nc.vector.tensor_tensor(t0, mvc[:, 0:1], mvc[:, 0:1], ALU.mult))
                nc.vector.tensor_tensor(mvc[:, 1:2], mvc[:, 1:2], t0, ALU.add).then_inc(s_gn0, 1)
                dve.wait_ge(s_gn0p, u + 1)
                link(nc.vector.tensor_copy(sc[:, 6:8], tiny[:, 0:2]))
                link(nc.vector.tensor_copy(m0, sc[:, 6:7]))
                link(nc.vector.tensor_tensor(t0, m0, m0, ALU.mult))
                link(nc.vector.tensor_tensor(v0, sc[:, 7:8], t0, ALU.subtract))
                nc.vector.tensor_scalar(v0, v0, 0.0, EPS, ALU.max, ALU.add).then_inc(s_var0, 1)
                dve.wait_ge(s_sq0, u + 1)
                link(nc.vector.reciprocal(r0, t0))
                link(nc.vector.tensor_scalar(nm0, m0, -1.0, None, ALU.mult))
                link(nc.vector.tensor_tensor(nmr0, nm0, r0, ALU.mult))
                link(nc.vector.tensor_scalar(wvs[:], wv2[:], r0, None, ALU.mult))
                link(nc.vector.tensor_scalar(wbs[:], wb2[:], r0, None, ALU.mult))
                nc.vector.tensor_copy(wvh[:], wvs[:])
                nc.vector.memset(nrun[:, RING - 1:RING], BIG)
                nc.vector.memset(mrun[:], 0.0).then_inc(s_w, 1)
                dve.wait_ge(s_bvp, u + 1)
                link(nc.vector.tensor_tensor(bvs[:], tiny[:, 4:5], bv_col[:], ALU.add))
                link(nc.vector.tensor_tensor(bbs[:], tiny[:, 5:6], bb_col[:], ALU.add))

                def add_block(bb, r):
                    now = slice(r % RING, r % RING + 1)
                    dve.wait_ge(s_m, bb + 1)
                    dve.wait_ge(s_al, bb + 1 + ACREDIT)
                    dve.wait_ge(s_ma, bb + ONE)
                    nc.vector.scalar_tensor_tensor(srun[:], srun[:], alpha[:, now], sblk[:, now], ALU.mult, ALU.add)
                    nc.vector.scalar_tensor_tensor(mrun[:], mrun[:], alpha[:, now], m_ps,
                                                   ALU.mult, ALU.add).then_inc(s_ma, 1)

                def max_b(k, r, before, after):
                    bb = NBLK * u + k
                    now, last = slice(r, r + 1), slice((r - 1) % RING, (r - 1) % RING + 1)
                    dve.wait_ge(s_b, bb + 1)
                    nc.vector.tensor_reduce(nblk[:, r % 2:r % 2 + 1], b_ps[r], AX.X, ALU.max,
                                            negate=True).then_inc(s_nblk, 1)
                    dve.wait_ge(s_nblk, 2 * bb + 1)
                    dve.wait_ge(s_al, bb - 2 + ACREDIT)
                    nc.vector.scalar_tensor_tensor(nrun[:, now], nblk[:, r % 2:r % 2 + 1], bbs[:, 0:1],
                                                   nrun[:, last], ALU.subtract, ALU.min).then_inc(s_nblk, 1)
                    dve.wait_ge(s_nblk, 2 * bb + 2)
                    nc.vector.tensor_tensor(bexp[:, now], nrun[:, now], bbs[:], ALU.add).then_inc(s_nm, 1)
                    if before(3):
                        add_block(bb - 3, r - 3)

                steps(dve, NBLK, RING, max_b)
                for k in range(NBLK - 3, NBLK):
                    add_block(NBLK * u + k, k)
                wait_alone(dve, s_ma, NBLK * (u + 1) + ONE)

                link(nc.vector.reciprocal(rsum[:], srun[:]))
                nc.vector.tensor_scalar(xbar[:], mrun[:], rsum[:], None, ALU.mult).then_inc(s_xbar, 1)
                dve.wait_ge(s_xbp, u + 1)
                for h in range(HPU):
                    d = slice(h * HEAD, (h + 1) * HEAD)
                    last = nc.vector.tensor_scalar(xbart[d, d], tiny[d, d], r0[d, :], nmr0[d, :], ALU.mult, ALU.add)
                last.then_inc(s_xbt, 1)
                dve.wait_ge(s_gp, u + 1)
                nc.vector.tensor_tensor(gaug[:, :, 0:HEAD], tiny[:, P:2 * P].rearrange("p (h m) -> p h m", h=HPU),
                                        ba_diag[:].rearrange("p (h m) -> p h m", h=HPU), ALU.add).then_inc(s_g, 1)

                def add_z(k, par):
                    bb = NBLK * u + k
                    dve.wait_ge(s_zz, bb + 1)
                    nc.vector.reciprocal(rinv[:].rearrange("p w h -> p (w h)"),
                                         z_ps[par][:, :, HEAD:HPU * (HEAD + 1):HEAD + 1]).then_inc(s_zn, 1)
                    dve.wait_ge(s_zn, 2 * bb + 1 + ZCREDIT)
                    zv = z_ps[par][:, :, 0:HPU * (HEAD + 1)].rearrange("p w (h m) -> p w h m", h=HPU)[:, :, :, 0:HEAD]
                    nc.vector.tensor_tensor(zs_[par][:], zv, rinv[:].unsqueeze(3).to_broadcast([P, WB, HPU, HEAD]),
                                            ALU.mult).then_inc(s_zn, 1)
                    dve.wait_ge(s_zn, 2 * bb + 2 + ZCREDIT)
                    xv = xh_wc[:, bass.ts(k, WB), :]
                    nc.vector.tensor_tensor(xv, xv, zs_[par][:].rearrange("p w h m -> p w (h m)"),
                                            ALU.add).then_inc(s_x1, 1)

                def max_v(k, r, before, after):
                    par = r % 2
                    dve.wait_ge(s_vt, NBLK * u + k + 1)
                    nc.vector.tensor_reduce(tmax[par][:].rearrange("p w h -> p (w h)"),
                                            vt_ps[par].rearrange("p (a n) -> p a n", n=HEAD), AX.X,
                                            ALU.max).then_inc(s_t, 1)
                    if before(2):
                        add_z(k - 2, par)

                steps(dve, NBLK, RING, max_v)
                add_z(NBLK - 2, 0)
                add_z(NBLK - 1, 1)
                wait_alone(dve, s_x1, NBLK * (u + 1))

                for gr in range(NG):
                    for q in range(4):
                        c = gr * GROUP + q * 4
                        last = nc.vector.bn_stats(sth[:, gr, q, :], xh[:, c:c + 4, :].rearrange("p c w -> p (c w)"))
                link(last)
                for gr in range(NG):
                    last = nc.vector.bn_aggr(mvh[:, gr, :], sth[:, gr, :, :].rearrange("p a b -> p (a b)"))
                link(last)
                link(nc.vector.tensor_tensor(v1[:], mvh[:, :, 0], mvh[:, :, 0], ALU.mult))
                nc.vector.tensor_tensor(mvh[:, :, 1], mvh[:, :, 1], v1[:], ALU.add).then_inc(s_gn1, 1)
                dve.wait_ge(s_gn1p, u + 1)
                t2 = tiny[:, 0:2 * NG].rearrange("p (g t) -> p g t", t=2)
                link(nc.vector.tensor_copy(m1[:], t2[:, :, 0]))
                link(nc.vector.tensor_tensor(v1[:], m1[:], m1[:], ALU.mult))
                link(nc.vector.tensor_tensor(v1[:], t2[:, :, 1], v1[:], ALU.subtract))
                nc.vector.tensor_scalar(v1[:], v1[:], 0.0, EPS, ALU.max, ALU.add).then_inc(s_var1, 1)
                dve.wait_ge(s_sq1, u + 1)
                link(nc.vector.reciprocal(r1[:], v1[:]))

                def norm(j, par, gr):
                    nc.vector.tensor_scalar(xn[:, par, :, :], xh[:, bass.ts(j, IMG), :], m1[:, bass.ds(gr, 1)],
                                            r1[:, bass.ds(gr, 1)], ALU.subtract, ALU.mult).then_inc(s_xn, 1)

                def add_out(g, j, half):
                    dve.wait_ge(s_op, 2 * g + half + 1)
                    v = xh[:, bass.ds(j * IMG + half * HALF, HALF), :].rearrange("p c w -> p (c w)")
                    nc.vector.tensor_tensor(v, o_ps, v, ALU.add).then_inc(s_o, 1)

                norm(0, 0, 0)
                norm(1, 1, 0)

                def remainder_rows(g, par):
                    dve.wait_ge(s_yr, g + 1)
                    v = yr[:, par, :]
                    nc.vector.scalar_tensor_tensor(v, v, SLOPE, v, ALU.mult, ALU.max).then_inc(s_yrc, 1)
                    dve.wait_ge(s_yrc, 3 * g + 1)
                    nc.vector.tensor_scalar(v, v, CLAMP, -CLAMP, ALU.min, ALU.max).then_inc(s_yrc, 1)
                    dve.wait_ge(s_yrc, 3 * g + 2)
                    nc.vector.tensor_tensor(yrb[:, par, :, :], v[:, 2 * P:UP].unsqueeze(2).to_broadcast([RR, REM, IMG]),
                                            own[:].unsqueeze(1).to_broadcast([RR, REM, IMG]), ALU.mult).then_inc(s_yrc, 1)

                def batch(j, par, before, after):
                    g = NBAT * u + j
                    for i in range(IMG):
                        v = yb[:, i % YRING, :, :]
                        dve.wait_ge(s_y, IMG * g + i + 1 + YCREDIT)
                        nc.vector.scalar_tensor_tensor(v, v, SLOPE, v, ALU.mult, ALU.max).then_inc(s_lr, 1)
                        dve.wait_ge(s_lr, IMG * g + i + 1)
                        nc.vector.tensor_scalar(yc[:, par, :, :, i], v[:, :, 2 * P:UP], CLAMP, -CLAMP, ALU.min, ALU.max)
                        nc.vector.tensor_scalar(v[:, :, 0:2 * P], v[:, :, 0:2 * P], CLAMP, -CLAMP, ALU.min,
                                                ALU.max).then_inc(s_yc, 1)
                        if i == 0:
                            remainder_rows(g, par)
                        if before(1) and i in (4, 6):
                            add_out(g - 1, j - 1, i // 6)
                        if more and i in (2, 3):
                            c_stats(2 * j + i - 2)
                        if after(2) and i == IMG - 1:
                            norm(j + 2, par, (j + 2) // 2)

                if more:
                    for q in range(XCH):
                        wait_alone(dve, s_xc[q], 16 * (u + 2))
                steps(dve, NBAT, 2, batch)
                for half in range(2):
                    add_out(NBAT * (u + 1) - 1, NBAT - 1, half)
                assert n[0] == N_SMALL, n[0]

            with dve.Fori(0, UNITS - 1) as u:
                unit(u, True)
            unit(UNITS - 1, False)

        @block.tensor
        def _(pe):
            def mm(o, l, r, start, stop=True, share=False):
                return nc.tensor.matmul(o, l, r, start=start, stop=stop, skip_group_check=share)

            pe.sem_inc(s_zrp, ONE)

            def unit(u):
                pe.wait_ge(s_gn0, u + 1)
                pe.wait_ge(s_z1, 2 * NBAT * u + ONE)
                mm(tiny[:, 0:2], avg_c[:], mvc[:], True).then_inc(s_gn0p, 1)
                pe.wait_ge(s_w, u + 1)
                mm(tiny[:, 5:6], wbs[:], nm0, True)
                mm(tiny[:, 4:5], wvs[:], nm0, True).then_inc(s_bvp, 1)

                def proj_b(k, r):
                    mm(b_ps[r % RING], wbs[:], xc_wh[:, bass.ts(k, WB), :], True).then_inc(s_b, 1)

                def sum_block(k, par):
                    bb = NBLK * u + k
                    pe.wait_ge(s_ptc, bb + 1)
                    pe.wait_ge(s_ma, bb + ONE)
                    for w in range(WB):
                        last = mm(m_ps, pt_[par][:, w * H:(w + 1) * H], xh_wc[:, WB * k + w, :], w == 0, w == WB - 1)
                    last.then_inc(s_m, 1)

                def attend(k, r, before, after):
                    par = r % 2
                    if after(2):
                        proj_b(k + 2, r + 2)
                    if before(2):
                        sum_block(k - 2, par)
                    pe.wait_ge(s_p, NBLK * u + k + 1)
                    for w in range(WB):
                        last = nc.tensor.transpose(pt_ps[par][:, w * H:(w + 1) * H], pe_[par][:, w * H:(w + 1) * H],
                                                   ident[:])
                    last.then_inc(s_pt, 1)

                pe.wait_ge(s_y, IMG * NBAT * u + YCREDIT)
                proj_b(0, 0)
                proj_b(1, 1)
                for i in range(2):
                    pe.wait_ge(s_xh[i], 16 * NBAT // 2 * (u + 1))
                steps(pe, NBLK, RING, attend)
                for k in (NBLK - 2, NBLK - 1):
                    sum_block(k, k % 2)

                pe.wait_ge(s_xbar, u + 1)
                nc.tensor.transpose(tiny[:, 0:P], xbar[:], ident[:]).then_inc(s_xbp, 1)
                pe.wait_ge(s_xbt, u + 1)
                mm(tiny[:, P:2 * P], xbart[:], wa2[:], True).then_inc(s_gp, 1)

                def v_t(k, par):
                    pe.wait_ge(s_xb, NBLK * u + k + 1)
                    mm(vt_ps[par], ones_row[:], bv_row4[:].rearrange("a w n -> a (w n)"), True)
                    for w in range(WB):
                        last = mm(vt_ps[par][:, w * P:(w + 1) * P], xb_[par][:, w, :], wvh[:], False, True,
                                  share=True)
                    last.then_inc(s_vt, 1)

                def z(k, par):
                    pe.wait_ge(s_e, NBLK * u + k + 1)
                    pe.wait_ge(s_zn, 2 * (NBLK * u + k - 2) + 2 + ZCREDIT)
                    for w in range(WB):
                        last = mm(z_ps[par][:, w, 0:HPU * (HEAD + 1)], ev_[par][:, w * H:(w + 1) * H],
                                  gaug[:].rearrange("p h m -> p (h m)"), True)
                    last.then_inc(s_zz, 1)

                def values(k, r, before, after):
                    par = r % 2
                    mm(v_ps[par], wvs[:], xc_wh[:, bass.ts(k, WB), :], True)
                    if before(1):
                        z(k - 1, 1 - par)
                    pe.wait_ge(s_ts, NBLK * u + k + 1)
                    for w in range(WB):
                        last = mm(v_ps[par][:, w * H:(w + 1) * H],
                                  tspr[par][:, w, :, :].rearrange("p h m -> p (h m)"), nident[:], False,
                                  True, share=True)
                    last.then_inc(s_v, 1)
                    if after(2):
                        v_t(k + 2, par)

                v_t(0, 0)
                v_t(1, 1)
                pe.wait_ge(s_g, u + 1)
                steps(pe, NBLK, RING, values)
                z(NBLK - 1, 1)

                pe.wait_ge(s_gn1, u + 1)
                mm(tiny[:, 0:2 * NG], avg_p[:], mvh[:].rearrange("p g t -> p (g t)"), True).then_inc(s_gn1p, 1)

                def up_rows(g, i, par):
                    if i == 0:
                        pe.wait_ge(s_xn, g + 1)
                    else:
                        pe.wait_ge(s_t1, IMG * g + i)
                    mm(s1_ps[:, 0:UP], xn[:, par, i, :], up_t[:], True).then_inc(s_s1, 1)

                def up_columns(g, i, par):
                    pe.wait_ge(s_y, IMG * g + i - 1 + YCREDIT)
                    for c in range(2):
                        last = mm(y_ps[i % 2][:, c, :], t1[:, par, c * P:(c + 1) * P, i], up_t[:], True)
                    last.then_inc(s_yp, 1)

                def down(o, la, lb, first):
                    mm(o[:, 0:DA], la, dn_t[:, DB - DA:DB], first, True, share=True)
                    return mm(o[:, DB0:H], lb, dn_t[:], False, True, share=True)

                def down_rows(g, i, par):
                    pe.wait_ge(s_yc, IMG * g + i + 1)
                    if i % HALF == 0:
                        pe.wait_ge(s_z1, 2 * g + i // HALF + ONE)
                    r = i % HALF
                    for c in range(2):
                        v = slice(c * P, (c + 1) * P)
                        down(dz_ps[:, c, r * H:(r + 1) * H], yb[:, i % YRING, 0, v], yb[:, i % YRING, 1, v], r == 0)
                    if r == HALF - 1:
                        half = i // HALF
                        pe.wait_ge(s_yrc, 3 * g + 3)
                        for c in range(2):
                            o = dz_ps[:, c, :].rearrange("p (r h) -> p r h", h=H)[:, :, H - DR:H]
                            last = mm(o, yr[:, par, c * P:(c + 1) * P], dn_r[:, half * HALF:(half + 1) * HALF, :], False,
                                      True, share=True)
                        last.then_inc(s_dz, 1)

                def down_columns(g, half):
                    pe.wait_ge(s_z1, 2 * g + half + 1 + ONE)
                    pe.wait_ge(s_zr, g + 1 + ONE)
                    pe.wait_ge(s_o, 2 * g + half + ONE)
                    for r in range(HALF):
                        down(o_ps[:, r * W:(r + 1) * W], z1[:, half, 0, r, :], z1[:, half, 1, r, :], r == 0)
                    o = o_ps.rearrange("p (r w) -> p r w", w=W)[:, :, W - DR:W]
                    mm(o, zr[:, :], dn_r[:, half * HALF:(half + 1) * HALF, :], False, True, share=True).then_inc(s_op, 1)

                def remainder_rows(g, par):
                    pe.wait_ge(s_t1, IMG * (g + 1))
                    mm(s1_ps[0:RR, 0:UP], t1[:, par, 2 * P:UP, :].rearrange("p q i -> p (q i)"), up_t[:],
                       True).then_inc(s_yrp, 1)

                def remainder_columns(g, par):
                    down(s1_ps[0:RR, :], yc[:, par, 0, :, :].rearrange("p q i -> p (q i)"),
                         yc[:, par, 1, :, :].rearrange("p q i -> p (q i)"), True)
                    mm(s1_ps[0:RR, H - DR:H], yrb[:, par, :, :].rearrange("p q i -> p (q i)"), dn_rs[:], False, True,
                       share=True).then_inc(s_zrp, 1)

                def batch(j, par, before, after):
                    g = NBAT * u + j
                    for i in range(IMG):
                        up_columns(g, i, par)
                        if after(1):
                            if i == 0:
                                pe.wait_ge(s_t1, IMG * (g + 1))
                            if i == 1:
                                pe.wait_ge(s_yr, g + 1)
                            if i == LAG and before(1):
                                pe.wait_ge(s_zr, g + ONE)
                            up_rows(g + 1, i, 1 - par)
                        if i >= LAG:
                            down_rows(g, i - LAG, par)
                        elif before(1):
                            down_rows(g - 1, IMG + i - LAG, 1 - par)
                        if i == 0:
                            if after(1):
                                pe.wait_ge(s_t1, IMG * (g + 1) + 1)
                            remainder_rows(g, par)
                        if before(1):
                            if i == LAG - 1:
                                if after(1):
                                    pe.wait_ge(s_t1, IMG * (g + 1) + LAG)
                                else:
                                    pe.wait_ge(s_yr, g + 1)
                                remainder_columns(g - 1, 1 - par)
                            if i in (3, 5):
                                down_columns(g - 1, i // 4)

                for i in range(IMG):
                    up_rows(NBAT * u, i, 0)
                steps(pe, NBAT, 2, batch)
                g = NBAT * (u + 1) - 1
                for i in range(IMG - LAG, IMG):
                    down_rows(g, i, 1)
                pe.wait_ge(s_zr, g + ONE)
                remainder_columns(g, 1)
                for half in range(2):
                    down_columns(g, half)

            pe.wait_ge(s_cst, 1)
            with pe.Fori(0, UNITS) as u:
                unit(u)


def kernel(x, L0_conv_Wa, L0_conv_ba, L0_conv_Wb, L0_conv_bb, L0_conv_Wv, L0_conv_bv, L1_conv_bias, L1_conv_up_filter,
           L1_conv_down_filter):
    import numpy as np
    import concourse.bacc as bacc
    from concourse.bass_utils import run_bass_kernel_spmd

    nc = bacc.Bacc("TRN2", target_bir_lowering=False, num_devices=1)
    host = {"x": x, "WaT": np.asarray(L0_conv_Wa).T, "ba": L0_conv_ba, "WbT": np.asarray(L0_conv_Wb).T,
            "bb": L0_conv_bb, "WvT": np.asarray(L0_conv_Wv).T, "bv": L0_conv_bv, "bias": L1_conv_bias, "fup": L1_conv_up_filter,
            "fdn": L1_conv_down_filter}
    arrays, args = {}, []
    for name, a in host.items():
        a = np.ascontiguousarray(a)
        arrays["in_" + name] = a
        args.append(nc.dram_tensor("in_" + name, a.shape, mybir.dt.from_np(a.dtype), kind="ExternalInput").ap())
    o = nc.dram_tensor("out_0", (B, C, H, W), mybir.dt.float32, kind="ExternalOutput").ap()
    attention_then_filters(nc, *args, o)
    r = run_bass_kernel_spmd(nc, [arrays], core_ids=[0])
    return r.results[0]["out_0"]
```

```python
import concourse.bass as bass
from concourse import mybir
from contextlib import ExitStack

B, C, H, W = 8, 512, 128, 128
P = 128
HEAD = 64
HPU = P // HEAD
UNITS = B * C // P
CPB = C // P
GROUP = C // 32
NG = P // GROUP
EPS = 1e-5
WB = 4
NBLK = W // WB
BS = WB * H
RING = 4
XCH = 4
IMG = 8
NBAT = P // IMG
YRING = 4
LAG = 2
HALF = IMG // 2
TAPS = 12
UP = 2 * H + 10
REM = UP - 2 * P
RR = IMG * REM
DA, DB = 64, 69
DB0 = H - DB
DR = 5
SLOPE, CLAMP = 0.2, 256.0
GAIN = 2.0 ** 0.5
UPGAIN = 4.0
BIG = 3.0e38
N_SMALL = 22


def attention_then_filters(nc, x, WaT, ba, WbT, bb_, WvT, bv, bias, fup, fdn, out):
    fp32, bf16, fp16 = mybir.dt.float32, mybir.dt.bfloat16, mybir.dt.float16
    ALU, ACT, AX = mybir.AluOpType, mybir.ActivationFunctionType, mybir.AxisListType

    x_ch = x.rearrange("b (u c) h w -> (b u) c (h w)", c=P)
    x_row = x.rearrange("b (u c) h w -> (b u) h c w", c=P)
    out_row = out.rearrange("b (u c) h w -> (b u) h c w", c=P)

    ctx = ExitStack()
    with ctx:
        def sb(name, shape, dt=fp32):
            return ctx.enter_context(nc.sbuf_tensor(name, shape, dt))

        def pb(name, shape, dt=fp32):
            return ctx.enter_context(nc.psum_tensor(name, shape, dt))

        def sem(name):
            return ctx.enter_context(nc.semaphore(name))

        xc = sb("xc", [P, H * W])
        xh = sb("xh", [P, P, W])
        xc_wh = xc[:, :].rearrange("c (h w) -> c w h", w=W)
        xh_wc = xh[:, :, :].rearrange("h c w -> h w c")
        ident = sb("ident", [P, P])
        nident = sb("nident", [P, P], bf16)
        avg_c = sb("avg_c", [P, P])
        avg_p = sb("avg_p", [P, P])
        wa2 = sb("wa2", [P, P])
        wb2 = sb("wb2", [P, P])
        wv2 = sb("wv2", [P, P])
        ba_diag = sb("ba_diag", [P, P])
        bb_col = sb("bb_col", [P, 1])
        bv_col = sb("bv_col", [P, 1])
        bv_row = sb("bv_row", [1, P])
        bv_row4 = sb("bv_row4", [1, WB, P], bf16)
        ones_row = sb("ones_row", [1, P], bf16)
        up_t = sb("up_t", [P, UP])
        dn_t = sb("dn_t", [P, DB])
        dn_r = sb("dn_r", [RR, IMG, DR])
        dn_rs = sb("dn_rs", [RR, DR])
        up_2 = sb("up_2", [P, 2, UP], fp16)
        dn_2 = sb("dn_2", [P, 2, DB], fp16)
        dr_2 = sb("dr_2", [RR, 2, IMG, DR], fp16)
        own = sb("own", [RR, IMG])
        f_up = sb("f_up", [P, TAPS])
        f_dn = sb("f_dn", [P, TAPS])
        bias_b = sb("bias_b", [P, C])
        bias_r = sb("bias_r", [RR, C // IMG])
        wbs = sb("wbs", [P, P])
        wvs = sb("wvs", [P, P])
        wvh = sb("wvh", [P, P], bf16)
        bvs = sb("bvs", [P, 1])
        bbs = sb("bbs", [P, 1])
        stc = sb("stc", [P, NBLK, 6])
        mvc = sb("mvc", [P, 2])
        sc = sb("sc", [P, 12])
        m0, nm0, r0, nmr0, v0, t0 = (sc[:, i:i + 1] for i in range(6))
        nblk = sb("nblk", [P, 2])
        nrun = sb("nrun", [P, RING])
        bexp = sb("bexp", [P, RING])
        alpha = sb("alpha", [P, RING])
        sblk = sb("sblk", [P, RING])
        srun = sb("srun", [P, 1])
        rsum = sb("rsum", [P, 1])
        mrun = sb("mrun", [P, P])
        xbar = sb("xbar", [P, P])
        xbart = sb("xbart", [P, P])
        gaug = sb("gaug", [P, HPU, HEAD + 1])
        pe_ = [sb(f"p{i}", [P, BS]) for i in range(2)]
        pt_ = [sb(f"pt{i}", [P, BS]) for i in range(2)]
        xb_ = [sb(f"xb{i}", [P, WB, P], bf16) for i in range(2)]
        ev_ = pe_
        tmax = [sb(f"tmax{i}", [P, WB, HPU], bf16) for i in range(2)]
        tspr = [sb(f"tspr{i}", [P, WB, HPU, HEAD], bf16) for i in range(2)]
        rinv = sb("rinv", [P, WB, HPU])
        zs_ = [t[:, :].rearrange("p (w h m) -> p w h m", w=WB, h=HPU) for t in pt_]
        sth = sb("sth", [P, NG, 4, 6])
        mvh = sb("mvh", [P, NG, 2])
        m1 = sb("m1", [P, NG])
        r1 = sb("r1", [P, NG])
        nmr1 = sb("nmr1", [P, NG])
        v1 = sb("v1", [P, NG])
        xn = sb("xn", [P, IMG, W])
        xn_2 = sb("xn_2", [P, 2, 2, IMG, W], fp16)
        t1 = sb("t1", [P, 2, 2, UP, IMG], fp16)
        yb = sb("yb", [P, YRING, 2, UP])
        yc = sb("yc", [P, 2, 2, REM, IMG])
        yr = sb("yr", [RR, 2, UP])
        yrb = sb("yrb", [RR, 2, REM, IMG])
        z1 = sb("z1", [P, 2, 2, 2, HALF, H], fp16)
        zr = sb("zr", [RR, 2, H], fp16)

        ps = pb("ps", [P, 8, 512])
        b_ps = [ps[:, i, :] for i in (0, 1, 6, 7)]
        pt_ps = [ps[:, i, :] for i in (2, 3)]
        m_ps = ps[:, 4, 0:P]
        tiny = ps[:, 5, :]
        v_ps = b_ps[0:2]
        z_ps = [ps[:, i:i + 2, :].rearrange("p b (w n) -> p (b w) n", w=2) for i in (2, 4)]
        vt_ps = [ps[:, i, :] for i in (6, 7)]
        y_ps = [ps[:, i:i + 2, 0:UP] for i in (0, 2)]
        dz_ps = [ps[:, i, :] for i in (4, 5)]
        s1_ps = ps[:, 6, :]
        o_ps = ps[:, 7, :]

        s_par = sem("parameters_loaded")
        s_zero = sem("zeros_set")
        s_mask = sem("masks_set")
        s_wz = sem("weights_zeroed")
        s_cst_dve = sem("constant_steps")
        s_cst = sem("constants_ready")
        s_xc = [sem(f"xc_piece{i}_loaded") for i in range(XCH)]
        s_xh = [sem(f"xh_loaded_{i}") for i in range(2)]
        s_st = [sem(f"out_stored_{i}") for i in range(2)]
        s_small = sem("vector_small_steps")
        s_gn0 = sem("norm0_stats_ready")
        s_gn0p = sem("norm0_averaged")
        s_var0 = sem("norm0_variance_ready")
        s_sq0 = sem("norm0_sqrt_ready")
        s_w = sem("scaled_weights_ready")
        s_bvp = sem("value_bias_product")
        s_b = sem("b_scores_in_psum")
        s_nblk = sem("block_max_ready")
        s_nm = sem("running_max_ready")
        s_p = sem("exp_b_ready")
        s_al = sem("alpha_ready")
        s_pt = sem("exp_b_transposed")
        s_ptc = sem("exp_b_transposed_copied")
        s_m = sem("block_sum_in_psum")
        s_ma = sem("block_sum_added")
        s_xbar = sem("xbar_ready")
        s_xbp = sem("xbar_transposed")
        s_xbt = sem("xbar_t_ready")
        s_gp = sem("g_in_psum")
        s_g = sem("g_ready")
        s_xb = sem("xc_bf16_ready")
        s_vt = sem("v_transposed_in_psum")
        s_t = sem("v_max_ready")
        s_ts = sem("v_max_spread")
        s_v = sem("v_in_psum")
        s_e = sem("exp_v_ready")
        s_zz = sem("z_in_psum")
        s_zn = sem("z_normalised")
        s_x1 = sem("x1_written")
        s_gn1 = sem("norm1_stats_ready")
        s_gn1p = sem("norm1_averaged")
        s_var1 = sem("norm1_variance_ready")
        s_sq1 = sem("norm1_sqrt_ready")
        s_xn = sem("xn_ready")
        s_s1 = sem("up_rows_in_psum")
        s_th = sem("up_rows_high")
        s_t1 = sem("up_rows_split")
        s_yp = sem("up_2d_in_psum")
        s_y = sem("up_2d_scaled")
        s_lr = sem("leaky_relu_done")
        s_yc = sem("clipped")
        s_yrp = sem("remainder_rows_in_psum")
        s_yr = sem("remainder_rows_scaled")
        s_yrc = sem("remainder_rows_clipped")
        s_dz = sem("down_rows_in_psum")
        s_zh = sem("down_rows_high")
        s_z1 = sem("down_rows_split")
        s_zrp = sem("remainder_columns_in_psum")
        s_zrh = sem("remainder_columns_high")
        s_zr = sem("remainder_columns_split")
        s_r1 = sem("norm1_scales_ready")
        s_xs = sem("xn_float32_ready")
        s_xnh = sem("xn_high_ready")
        s_op = sem("output_in_psum")
        s_o = sem("output_added")

        ZCREDIT = 4
        s_alone = sem("lone_waits")

        ACREDIT = 3
        DCREDIT = 2
        OCREDIT = 3
        ONE = 1
        YCREDIT = 2

        block = ctx.enter_context(nc.Block())

        def wait_alone(eng, semaphore, value):
            eng.wait_ge(semaphore, value)
            eng.sem_inc(s_alone, 1)

        def steps(eng, n, unroll, step):
            for r in range(unroll):
                step(r, r, lambda b: r >= b, lambda a: True)
            with eng.Fori(1, n // unroll - 1) as k:
                for r in range(unroll):
                    step(unroll * k + r, r, lambda b: True, lambda a: True)
            for r in range(unroll):
                step(n - unroll + r, r, lambda b: True, lambda a: r + a < unroll)

        @block.sync
        def _(sp):
            def load_xc(u):
                n = H * W // XCH
                for i in range(XCH):
                    sp.dma_start(xc[:, i * n:(i + 1) * n], x_ch[u, :, i * n:(i + 1) * n]).then_inc(s_xc[i], 16)

            def load_xh(u, j, par):
                sp.dma_start(xh[:, bass.ts(j, IMG), :], x_row[u, :, bass.ts(j, IMG), :]).then_inc(s_xh[par], 16)

            load_xc(0)
            sp.dma_start(f_up[:, :], fup.rearrange("(a n) -> a n", a=1).to_broadcast([P, TAPS])).then_inc(s_par, 16)
            sp.dma_start(f_dn[:, :], fdn.rearrange("(a n) -> a n", a=1).to_broadcast([P, TAPS])).then_inc(s_par, 16)
            sp.dma_start(bias_b[:, :], bias.rearrange("(a n) -> a n", a=1).to_broadcast([P, C])).then_inc(s_par, 16)
            sp.dma_start(bv_row[:, :].rearrange("a (t n) -> a t n", t=HPU),
                         bv.rearrange("(a t n) -> a t n", a=1, t=1).to_broadcast([1, HPU, HEAD])).then_inc(s_par, 16)
            sp.wait_ge(s_wz, 1)
            for h in range(HPU):
                d = slice(h * HEAD, (h + 1) * HEAD)
                for dst, src in ((wa2, WaT), (wb2, WbT), (wv2, WvT)):
                    sp.dma_start(dst[d, d], src).then_inc(s_par, 16)
                sp.dma_start(ba_diag[d, d], ba.rearrange("(a n) -> a n", a=1).to_broadcast([HEAD, HEAD])).then_inc(s_par, 16)
                sp.dma_start(bb_col[d, :], bb_.rearrange("(n a) -> n a", a=1)).then_inc(s_par, 16)
                sp.dma_start(bv_col[d, :], bv.rearrange("(n a) -> n a", a=1)).then_inc(s_par, 16)
            for i in range(REM):
                sp.dma_start(bias_r[i * IMG:(i + 1) * IMG, :], bias.rearrange("(t n) -> n t", n=IMG),
                             allow_slow_non_contiguous=True).then_inc(s_par, 16)
            sp.wait_ge(s_cst, 1)
            for j in range(NBAT):
                load_xh(0, j, j % 2)

            def unit(u, more):
                if more:
                    wait_alone(sp, s_v, NBLK * (u + 1))
                    wait_alone(sp, s_xb, NBLK * (u + 1))
                    load_xc(u + 1)

                def batch(j, par, before, after):
                    wait_alone(sp, s_o, 2 * (NBAT * u + j + 1) + OCREDIT)
                    sp.dma_start(out_row[u, :, bass.ts(j, IMG), :], xh[:, bass.ts(j, IMG), :]).then_inc(s_st[par], 16)
                    if before(1):
                        wait_alone(sp, s_st[1 - par], 16 * (NBAT // 2 * u + (j - 1) // 2 + 1))
                        if more:
                            load_xh(u + 1, j - 1, 1 - par)

                steps(sp, NBAT, 2, batch)
                wait_alone(sp, s_st[1], 16 * (NBAT // 2 * (u + 1)))
                if more:
                    load_xh(u + 1, NBAT - 1, 1)

            with sp.Fori(0, UNITS - 1) as u:
                unit(u, True)
            unit(UNITS - 1, False)

        @block.gpsimd
        def _(pool):
            yflat = xh[:, 0:TAPS * UP // W + 1, :].rearrange("p a b -> p (a b)")
            tflat = yb[:, :, :, :].rearrange("p a b c -> p (a b c)")
            nc.gpsimd.memset(wa2[:], 0.0)
            nc.gpsimd.memset(wb2[:], 0.0)
            nc.gpsimd.memset(wv2[:], 0.0)
            nc.gpsimd.memset(ba_diag[:], 0.0).then_inc(s_wz, 1)
            nc.gpsimd.memset(yflat, 0.0)
            nc.gpsimd.memset(tflat, 0.0)
            nc.gpsimd.memset(ident[:], 0.0)
            nc.gpsimd.memset(nident[:], 0.0)
            nc.gpsimd.memset(avg_c[:], 1.0 / GROUP).then_inc(s_zero, 1)
            pool.wait_ge(s_zero, 1)
            nc.gpsimd.affine_select(out=yflat[:, 0:TAPS * UP].rearrange("p (k u) -> p k u", k=TAPS),
                                    in_=yflat[:, 0:TAPS * UP].rearrange("p (k u) -> p k u", k=TAPS),
                                    compare_op=ALU.not_equal, fill=1.0, base=0,
                                    pattern=[[1, TAPS], [-1, UP]], channel_multiplier=2)
            nc.gpsimd.affine_select(out=tflat[:, 0:TAPS * DB].rearrange("p (k u) -> p k u", k=TAPS),
                                    in_=tflat[:, 0:TAPS * DB].rearrange("p (k u) -> p k u", k=TAPS),
                                    compare_op=ALU.not_equal, fill=1.0, base=-1,
                                    pattern=[[1, TAPS], [-2, DB]], channel_multiplier=1)
            mr = tflat[0:RR, TAPS * DB:TAPS * (DB + IMG * DR)].rearrange("p (k i q) -> p k i q", k=TAPS, i=IMG)
            o = TAPS * (DB + IMG * DR)
            mo = tflat[0:RR, o:o + IMG * REM].rearrange("p (i q) -> p i q", i=IMG)
            nc.gpsimd.affine_select(out=mr, in_=mr, compare_op=ALU.not_equal, fill=1.0, base=-IMG,
                                    pattern=[[IMG, TAPS], [-1, IMG], [-2 * IMG, DR]], channel_multiplier=1)
            nc.gpsimd.affine_select(out=mo, in_=mo, compare_op=ALU.not_equal, fill=1.0, base=0,
                                    pattern=[[-1, IMG], [-IMG, REM]], channel_multiplier=1)
            nc.gpsimd.affine_select(out=ident[:], in_=ident[:], compare_op=ALU.not_equal, fill=1.0, base=0,
                                    pattern=[[-1, P]], channel_multiplier=1)
            nc.gpsimd.affine_select(out=nident[:], in_=nident[:], compare_op=ALU.not_equal, fill=-1.0, base=0,
                                    pattern=[[-1, P]], channel_multiplier=1).then_inc(s_zero, 1)
            pool.wait_ge(s_zero, 2)
            a3 = avg_c[:].rearrange("p (g c) -> p g c", c=GROUP)
            nc.gpsimd.affine_select(out=a3, in_=a3, compare_op=ALU.is_ge, fill=0.0, base=0,
                                    pattern=[[-GROUP, NG], [0, GROUP]], channel_multiplier=1).then_inc(s_zero, 1)
            pool.wait_ge(s_zero, 3)
            nc.gpsimd.affine_select(out=a3, in_=a3, compare_op=ALU.is_ge, fill=0.0, base=GROUP - 1,
                                    pattern=[[GROUP, NG], [0, GROUP]], channel_multiplier=-1).then_inc(s_mask, 1)

            def spread(k, par):
                wait_alone(pool, s_t, k + 1)
                nc.gpsimd.tensor_copy(tspr[par][:], tmax[par][:].unsqueeze(3).to_broadcast([P, WB, HPU, HEAD])).then_inc(s_ts, 1)

            with pool.Fori(0, UNITS * NBLK // 2) as k:
                spread(2 * k, 0)
                spread(2 * k + 1, 1)

        @block.scalar
        def _(act):
            act.sem_inc(s_y, YCREDIT)
            act.sem_inc(s_al, ACREDIT)

            def unit(u):
                act.wait_ge(s_var0, u + 1)
                act.activation(t0, v0, ACT.Sqrt).then_inc(s_sq0, 1)

                def exp_b(k, r, before, after):
                    now, last = slice(r, r + 1), slice((r - 1) % RING, (r - 1) % RING + 1)
                    act.wait_ge(s_nm, NBLK * u + k + 1)
                    act.activation(alpha[:, now], nrun[:, last], ACT.Exp, scale=-1.0,
                                   bias=nrun[:, now]).then_inc(s_al, 1)
                    act.activation(pe_[r % 2][:, :], b_ps[r], ACT.Exp, bias=bexp[:, now],
                                   accum_out=sblk[:, now]).then_inc(s_p, 1)
                    if before(1):
                        act.wait_ge(s_pt, NBLK * u + k)
                        act.activation(pt_[1 - r % 2][:, :], pt_ps[1 - r % 2], ACT.Copy).then_inc(s_ptc, 1)

                steps(act, NBLK, RING, exp_b)
                act.wait_ge(s_pt, NBLK * (u + 1))
                act.activation(pt_[1][:, :], pt_ps[1], ACT.Copy).then_inc(s_ptc, 1)

                def to_bf16(k, par):
                    act.activation(xb_[par][:, :, :], xc_wh[:, bass.ts(k, WB), :], ACT.Identity,
                                   bias=nm0).then_inc(s_xb, 1)

                def exp_v(k, r, before, after):
                    par = r % 2
                    if after(2):
                        act.wait_ge(s_vt, NBLK * u + k + 1)
                        to_bf16(k + 2, par)
                    act.wait_ge(s_v, NBLK * u + k + 1)
                    act.activation(ev_[par][:, :], v_ps[par], ACT.Exp, bias=bvs[:, 0:1]).then_inc(s_e, 1)

                to_bf16(0, 0)
                to_bf16(1, 1)
                steps(act, NBLK, RING, exp_v)

                act.wait_ge(s_var1, u + 1)
                act.activation(v1[:, :], v1[:, :], ACT.Sqrt).then_inc(s_sq1, 1)

                def t1_high(g, i, par):
                    act.wait_ge(s_s1, IMG * g + i + 1)
                    act.activation(t1[:, par, 0, :, i], s1_ps[:, 0:UP], ACT.Copy).then_inc(s_th, 1)

                def xn_high(j, par, gr):
                    act.activation(xn_2[:, par, 0, :, :], xh[:, bass.ts(j, IMG), :], ACT.Identity,
                                   scale=r1[:, bass.ds(gr, 1)], bias=nmr1[:, bass.ds(gr, 1)]).then_inc(s_xnh, 1)

                def down_high(g, half):
                    for c in range(2):
                        act.wait_ge(s_dz, 4 * g + 2 * half + c + 1)
                        act.activation(z1[:, half, 0, c, :, :].rearrange("p a b -> p (a b)"), dz_ps[c],
                                       ACT.Copy).then_inc(s_zh, 1)

                def remainder_high(g):
                    act.wait_ge(s_zrp, g + 1 + ONE)
                    act.activation(zr[:, 0, :], o_ps[0:RR, 0:H], ACT.Copy).then_inc(s_zrh, 1)

                def batch(j, par, before, after):
                    g = NBAT * u + j
                    c0 = (u % CPB) * P + j * IMG
                    for i in range(IMG):
                        act.wait_ge(s_yp, IMG * g + i + 1)
                        act.activation(yb[:, i % YRING, :, :], y_ps[i % 2], ACT.Identity, scale=UPGAIN * GAIN,
                                       bias=bias_b[:, bass.ds(c0 + i, 1)]).then_inc(s_y, 1)
                        if after(1):
                            t1_high(g + 1, i, 1 - par)
                        if i == 0:
                            act.wait_ge(s_yrp, g + 1)
                            act.activation(yr[:, par, :], o_ps[0:RR, 0:UP], ACT.Identity, scale=UPGAIN * GAIN,
                                           bias=bias_r[:, bass.ds((u % CPB) * NBAT + j, 1)]).then_inc(s_yr, 1)
                        if i == LAG - 1 and before(1):
                            down_high(g - 1, 1)
                            remainder_high(g - 1)
                        if i == LAG and after(2):
                            xn_high(j + 2, par, (j + 2) // 2)
                        if i == HALF - 1 + LAG:
                            down_high(g, 0)

                act.wait_ge(s_r1, u + 1)
                xn_high(0, 0, 0)
                xn_high(1, 1, 0)
                for i in range(IMG):
                    t1_high(NBAT * u, i, 0)
                steps(act, NBAT, 2, batch)
                down_high(NBAT * (u + 1) - 1, 1)
                remainder_high(NBAT * (u + 1) - 1)

            act.wait_ge(s_cst, 1)
            with act.Fori(0, UNITS) as u:
                unit(u)

        @block.vector
        def _(dve):
            def c_stats(k):
                return nc.vector.bn_stats(stc[:, bass.ds(k, 1), :].rearrange("p a b -> p (a b)"), xc[:, bass.ts(k, 512)])

            dve.sem_inc(s_zn, ZCREDIT)
            dve.sem_inc(s_z1, DCREDIT)
            dve.sem_inc(s_o, OCREDIT)
            for started in (s_ma, s_zr):
                dve.sem_inc(started, ONE)
            n_par = 4 + 6 * HPU + REM
            dve.wait_ge(s_par, 16 * n_par)
            dve.wait_ge(s_mask, 1)
            yflat = xh[:, 0:TAPS * UP // W + 1, :].rearrange("p a b -> p (a b)")
            tflat = yb[:, :, :, :].rearrange("p a b c -> p (a b c)")
            nc.vector.memset(avg_p[:], 1.0 / P)
            nc.vector.memset(ones_row[:], 1.0)
            nc.vector.memset(gaug[:], 0.0)
            nc.vector.memset(xbart[:], 0.0)
            nc.vector.tensor_scalar(bias_b[:], bias_b[:], GAIN, None, ALU.mult)
            nc.vector.tensor_scalar(bias_r[:], bias_r[:], GAIN, None, ALU.mult)
            for w in range(WB):
                nc.vector.tensor_copy(bv_row4[:, w, :], bv_row[:, :])
            nc.vector.memset(up_t[:], 0.0)
            nc.vector.memset(dn_t[:], 0.0)
            nc.vector.memset(dn_r[:], 0.0).then_inc(s_cst_dve, 1)
            for k in range(TAPS):
                dve.wait_ge(s_cst_dve, k + 1)
                nc.vector.scalar_tensor_tensor(up_t[:], yflat[:, k * UP:(k + 1) * UP], f_up[:, k:k + 1], up_t[:],
                                               ALU.mult, ALU.add)
                nc.vector.scalar_tensor_tensor(dn_t[:], tflat[:, k * DB:(k + 1) * DB], f_dn[:, k:k + 1], dn_t[:],
                                               ALU.mult, ALU.add)
                o = TAPS * DB + k * IMG * DR
                nc.vector.scalar_tensor_tensor(dn_r[:].rearrange("p i q -> p (i q)"), tflat[0:RR, o:o + IMG * DR],
                                               f_dn[0:RR, k:k + 1], dn_r[:].rearrange("p i q -> p (i q)"),
                                               ALU.mult, ALU.add).then_inc(s_cst_dve, 1)
            for h in range(HPU):
                nc.vector.memset(gaug[h * HEAD:(h + 1) * HEAD, h, HEAD:HEAD + 1], 1.0)
            o = TAPS * (DB + IMG * DR)
            nc.vector.tensor_reduce(own[:], tflat[0:RR, o:o + IMG * REM].rearrange("p (i q) -> p i q", i=IMG), AX.X,
                                    ALU.add)
            dve.wait_ge(s_cst_dve, TAPS + 1)
            nc.vector.tensor_reduce(dn_rs[:], dn_r[:].rearrange("p i q -> p q i"), AX.X, ALU.add)
            dr = dn_r[:].rearrange("p i q -> p (i q)")
            drh, drl = (dr_2[:, i, :, :].rearrange("p i q -> p (i q)") for i in range(2))
            nc.vector.tensor_copy(up_2[:, 0, :], up_t[:])
            nc.vector.tensor_copy(dn_2[:, 0, :], dn_t[:])
            nc.vector.tensor_copy(drh, dr).then_inc(s_cst_dve, 1)
            dve.wait_ge(s_cst_dve, TAPS + 2)
            nc.vector.tensor_tensor(up_2[:, 1, :], up_t[:], up_2[:, 0, :], ALU.subtract)
            nc.vector.tensor_tensor(dn_2[:, 1, :], dn_t[:], dn_2[:, 0, :], ALU.subtract)
            nc.vector.tensor_tensor(drl, dr, drh, ALU.subtract).then_inc(s_cst, 1)
            for i in range(XCH):
                dve.wait_ge(s_xc[i], 16)
            with dve.Fori(0, NBLK) as k:
                c_stats(k)

            def unit(u, more):
                n = [0]

                def link(ins):
                    ins.then_inc(s_small, 1)
                    n[0] += 1
                    wait_alone(dve, s_small, N_SMALL * u + n[0])

                link(nc.vector.memset(srun[:], 0.0))
                link(nc.vector.bn_aggr(mvc[:], stc[:].rearrange("p a b -> p (a b)")))
                link(nc.vector.tensor_tensor(t0, mvc[:, 0:1], mvc[:, 0:1], ALU.mult))
                nc.vector.tensor_tensor(mvc[:, 1:2], mvc[:, 1:2], t0, ALU.add).then_inc(s_gn0, 1)
                dve.wait_ge(s_gn0p, u + 1)
                link(nc.vector.tensor_copy(sc[:, 6:8], tiny[:, 0:2]))
                link(nc.vector.tensor_copy(m0, sc[:, 6:7]))
                link(nc.vector.tensor_tensor(t0, m0, m0, ALU.mult))
                link(nc.vector.tensor_tensor(v0, sc[:, 7:8], t0, ALU.subtract))
                nc.vector.tensor_scalar(v0, v0, 0.0, EPS, ALU.max, ALU.add).then_inc(s_var0, 1)
                dve.wait_ge(s_sq0, u + 1)
                link(nc.vector.reciprocal(r0, t0))
                link(nc.vector.tensor_scalar(nm0, m0, -1.0, None, ALU.mult))
                link(nc.vector.tensor_tensor(nmr0, nm0, r0, ALU.mult))
                link(nc.vector.tensor_scalar(wvs[:], wv2[:], r0, None, ALU.mult))
                link(nc.vector.tensor_scalar(wbs[:], wb2[:], r0, None, ALU.mult))
                nc.vector.tensor_copy(wvh[:], wvs[:])
                nc.vector.memset(nrun[:, RING - 1:RING], BIG)
                nc.vector.memset(mrun[:], 0.0).then_inc(s_w, 1)
                dve.wait_ge(s_bvp, u + 1)
                link(nc.vector.tensor_tensor(bvs[:], tiny[:, 4:5], bv_col[:], ALU.add))
                link(nc.vector.tensor_tensor(bbs[:], tiny[:, 5:6], bb_col[:], ALU.add))

                def add_block(bb, r):
                    now = slice(r % RING, r % RING + 1)
                    dve.wait_ge(s_m, bb + 1)
                    dve.wait_ge(s_al, bb + 1 + ACREDIT)
                    dve.wait_ge(s_ma, bb + ONE)
                    nc.vector.scalar_tensor_tensor(srun[:], srun[:], alpha[:, now], sblk[:, now], ALU.mult, ALU.add)
                    nc.vector.scalar_tensor_tensor(mrun[:], mrun[:], alpha[:, now], m_ps,
                                                   ALU.mult, ALU.add).then_inc(s_ma, 1)

                def max_b(k, r, before, after):
                    bb = NBLK * u + k
                    now, last = slice(r, r + 1), slice((r - 1) % RING, (r - 1) % RING + 1)
                    dve.wait_ge(s_b, bb + 1)
                    nc.vector.tensor_reduce(nblk[:, r % 2:r % 2 + 1], b_ps[r], AX.X, ALU.max,
                                            negate=True).then_inc(s_nblk, 1)
                    dve.wait_ge(s_nblk, 2 * bb + 1)
                    dve.wait_ge(s_al, bb - 2 + ACREDIT)
                    nc.vector.scalar_tensor_tensor(nrun[:, now], nblk[:, r % 2:r % 2 + 1], bbs[:, 0:1],
                                                   nrun[:, last], ALU.subtract, ALU.min).then_inc(s_nblk, 1)
                    dve.wait_ge(s_nblk, 2 * bb + 2)
                    nc.vector.tensor_tensor(bexp[:, now], nrun[:, now], bbs[:], ALU.add).then_inc(s_nm, 1)
                    if before(3):
                        add_block(bb - 3, r - 3)

                steps(dve, NBLK, RING, max_b)
                for k in range(NBLK - 3, NBLK):
                    add_block(NBLK * u + k, k)
                wait_alone(dve, s_ma, NBLK * (u + 1) + ONE)

                link(nc.vector.reciprocal(rsum[:], srun[:]))
                nc.vector.tensor_scalar(xbar[:], mrun[:], rsum[:], None, ALU.mult).then_inc(s_xbar, 1)
                dve.wait_ge(s_xbp, u + 1)
                for h in range(HPU):
                    d = slice(h * HEAD, (h + 1) * HEAD)
                    last = nc.vector.tensor_scalar(xbart[d, d], tiny[d, d], r0[d, :], nmr0[d, :], ALU.mult, ALU.add)
                last.then_inc(s_xbt, 1)
                dve.wait_ge(s_gp, u + 1)
                nc.vector.tensor_tensor(gaug[:, :, 0:HEAD], tiny[:, P:2 * P].rearrange("p (h m) -> p h m", h=HPU),
                                        ba_diag[:].rearrange("p (h m) -> p h m", h=HPU), ALU.add).then_inc(s_g, 1)

                def add_z(k, par):
                    bb = NBLK * u + k
                    dve.wait_ge(s_zz, bb + 1)
                    nc.vector.reciprocal(rinv[:].rearrange("p w h -> p (w h)"),
                                         z_ps[par][:, :, HEAD:HPU * (HEAD + 1):HEAD + 1]).then_inc(s_zn, 1)
                    dve.wait_ge(s_zn, 2 * bb + 1 + ZCREDIT)
                    zv = z_ps[par][:, :, 0:HPU * (HEAD + 1)].rearrange("p w (h m) -> p w h m", h=HPU)[:, :, :, 0:HEAD]
                    nc.vector.tensor_tensor(zs_[par][:], zv, rinv[:].unsqueeze(3).to_broadcast([P, WB, HPU, HEAD]),
                                            ALU.mult).then_inc(s_zn, 1)
                    dve.wait_ge(s_zn, 2 * bb + 2 + ZCREDIT)
                    xv = xh_wc[:, bass.ts(k, WB), :]
                    nc.vector.tensor_tensor(xv, xv, zs_[par][:].rearrange("p w h m -> p w (h m)"),
                                            ALU.add).then_inc(s_x1, 1)

                def max_v(k, r, before, after):
                    par = r % 2
                    dve.wait_ge(s_vt, NBLK * u + k + 1)
                    nc.vector.tensor_reduce(tmax[par][:].rearrange("p w h -> p (w h)"),
                                            vt_ps[par].rearrange("p (a n) -> p a n", n=HEAD), AX.X,
                                            ALU.max).then_inc(s_t, 1)
                    if before(2):
                        add_z(k - 2, par)

                steps(dve, NBLK, RING, max_v)
                add_z(NBLK - 2, 0)
                add_z(NBLK - 1, 1)
                wait_alone(dve, s_x1, NBLK * (u + 1))

                for gr in range(NG):
                    for q in range(4):
                        c = gr * GROUP + q * 4
                        last = nc.vector.bn_stats(sth[:, gr, q, :], xh[:, c:c + 4, :].rearrange("p c w -> p (c w)"))
                link(last)
                for gr in range(NG):
                    last = nc.vector.bn_aggr(mvh[:, gr, :], sth[:, gr, :, :].rearrange("p a b -> p (a b)"))
                link(last)
                link(nc.vector.tensor_tensor(v1[:], mvh[:, :, 0], mvh[:, :, 0], ALU.mult))
                nc.vector.tensor_tensor(mvh[:, :, 1], mvh[:, :, 1], v1[:], ALU.add).then_inc(s_gn1, 1)
                dve.wait_ge(s_gn1p, u + 1)
                t2 = tiny[:, 0:2 * NG].rearrange("p (g t) -> p g t", t=2)
                link(nc.vector.tensor_copy(m1[:], t2[:, :, 0]))
                link(nc.vector.tensor_tensor(v1[:], m1[:], m1[:], ALU.mult))
                link(nc.vector.tensor_tensor(v1[:], t2[:, :, 1], v1[:], ALU.subtract))
                nc.vector.tensor_scalar(v1[:], v1[:], 0.0, EPS, ALU.max, ALU.add).then_inc(s_var1, 1)
                dve.wait_ge(s_sq1, u + 1)
                link(nc.vector.reciprocal(r1[:], v1[:]))
                nc.vector.scalar_tensor_tensor(nmr1[:], m1[:], -1.0, r1[:], ALU.mult, ALU.mult).then_inc(s_r1, 1)

                def norm(j, gr):
                    nc.vector.tensor_scalar(xn[:], xh[:, bass.ts(j, IMG), :], m1[:, bass.ds(gr, 1)],
                                            r1[:, bass.ds(gr, 1)], ALU.subtract, ALU.mult).then_inc(s_xs, 1)

                def norm_low(j, par):
                    dve.wait_ge(s_xnh, NBAT * u + j + 1)
                    dve.wait_ge(s_xs, NBAT * u + j + 1)
                    nc.vector.tensor_tensor(xn_2[:, par, 1, :, :], xn[:], xn_2[:, par, 0, :, :],
                                            ALU.subtract).then_inc(s_xn, 1)

                def t1_low(g, i, par):
                    dve.wait_ge(s_th, IMG * g + i + 1)
                    nc.vector.tensor_tensor(t1[:, par, 1, :, i], s1_ps[:, 0:UP], t1[:, par, 0, :, i],
                                            ALU.subtract).then_inc(s_t1, 1)

                def down_low(g, half, c):
                    dve.wait_ge(s_zh, 4 * g + 2 * half + c + 1)
                    lo, hi = (z1[:, half, i, c, :, :].rearrange("p a b -> p (a b)") for i in (1, 0))
                    nc.vector.tensor_tensor(lo, dz_ps[c], hi, ALU.subtract).then_inc(s_z1, 1)

                def remainder_low(g):
                    dve.wait_ge(s_zrh, g + 1)
                    nc.vector.tensor_tensor(zr[:, 1, :], o_ps[0:RR, 0:H], zr[:, 0, :], ALU.subtract).then_inc(s_zr, 1)

                def add_out(g, j, half):
                    dve.wait_ge(s_op, 2 * g + half + 1)
                    v = xh[:, bass.ds(j * IMG + half * HALF, HALF), :].rearrange("p c w -> p (c w)")
                    nc.vector.tensor_tensor(v, o_ps, v, ALU.add).then_inc(s_o, 1)

                for j in range(2):
                    if j:
                        wait_alone(dve, s_xn, NBAT * u + 1)
                    norm(j, 0)
                    norm_low(j, j)
                for i in range(IMG):
                    t1_low(NBAT * u, i, 0)

                def remainder_rows(g, par):
                    dve.wait_ge(s_yr, g + 1)
                    v = yr[:, par, :]
                    nc.vector.scalar_tensor_tensor(v, v, SLOPE, v, ALU.mult, ALU.max).then_inc(s_yrc, 1)
                    dve.wait_ge(s_yrc, 3 * g + 1)
                    nc.vector.tensor_scalar(v, v, CLAMP, -CLAMP, ALU.min, ALU.max).then_inc(s_yrc, 1)
                    dve.wait_ge(s_yrc, 3 * g + 2)
                    nc.vector.tensor_tensor(yrb[:, par, :, :], v[:, 2 * P:UP].unsqueeze(2).to_broadcast([RR, REM, IMG]),
                                            own[:].unsqueeze(1).to_broadcast([RR, REM, IMG]), ALU.mult).then_inc(s_yrc, 1)

                def batch(j, par, before, after):
                    g = NBAT * u + j
                    for i in range(IMG):
                        v = yb[:, i % YRING, :, :]
                        dve.wait_ge(s_y, IMG * g + i + 1 + YCREDIT)
                        nc.vector.scalar_tensor_tensor(v, v, SLOPE, v, ALU.mult, ALU.max).then_inc(s_lr, 1)
                        if after(1):
                            t1_low(g + 1, i, 1 - par)
                        dve.wait_ge(s_lr, IMG * g + i + 1)
                        nc.vector.tensor_scalar(yc[:, par, :, :, i], v[:, :, 2 * P:UP], CLAMP, -CLAMP, ALU.min, ALU.max)
                        nc.vector.tensor_scalar(v[:, :, 0:2 * P], v[:, :, 0:2 * P], CLAMP, -CLAMP, ALU.min,
                                                ALU.max).then_inc(s_yc, 1)
                        if i == 0:
                            remainder_rows(g, par)
                        if i == LAG - 1 and before(1):
                            for c in range(2):
                                down_low(g - 1, 1, c)
                            remainder_low(g - 1)
                        if i == HALF - 1 + LAG:
                            for c in range(2):
                                down_low(g, 0, c)
                        if before(1) and i in (4, 6):
                            add_out(g - 1, j - 1, i // 6)
                        if more and i in (4, 7):
                            c_stats(2 * j + i // 7)
                        if after(2) and i == 2:
                            norm(j + 2, (j + 2) // 2)
                        if after(2) and i == 3:
                            norm_low(j + 2, par)

                if more:
                    for q in range(XCH):
                        wait_alone(dve, s_xc[q], 16 * (u + 2))
                steps(dve, NBAT, 2, batch)
                for c in range(2):
                    down_low(NBAT * (u + 1) - 1, 1, c)
                remainder_low(NBAT * (u + 1) - 1)
                for half in range(2):
                    add_out(NBAT * (u + 1) - 1, NBAT - 1, half)
                assert n[0] == N_SMALL, n[0]

            with dve.Fori(0, UNITS - 1) as u:
                unit(u, True)
            unit(UNITS - 1, False)

        @block.tensor
        def _(pe):
            def mm(o, l, r, start, stop=True, share=False):
                return nc.tensor.matmul(o, l, r, start=start, stop=stop, skip_group_check=share)

            def mm3(o, lh, ll, rh, rl, first):
                mm(o, lh, rh, first, True, share=True)
                mm(o, lh, rl, False, True, share=True)
                return mm(o, ll, rh, False, True, share=True)

            pe.sem_inc(s_zrp, ONE)

            def unit(u):
                pe.wait_ge(s_gn0, u + 1)
                pe.wait_ge(s_z1, 4 * NBAT * u + DCREDIT)
                mm(tiny[:, 0:2], avg_c[:], mvc[:], True).then_inc(s_gn0p, 1)
                pe.wait_ge(s_w, u + 1)
                mm(tiny[:, 5:6], wbs[:], nm0, True)
                mm(tiny[:, 4:5], wvs[:], nm0, True).then_inc(s_bvp, 1)

                def proj_b(k, r):
                    mm(b_ps[r % RING], wbs[:], xc_wh[:, bass.ts(k, WB), :], True).then_inc(s_b, 1)

                def sum_block(k, par):
                    bb = NBLK * u + k
                    pe.wait_ge(s_ptc, bb + 1)
                    pe.wait_ge(s_ma, bb + ONE)
                    for w in range(WB):
                        last = mm(m_ps, pt_[par][:, w * H:(w + 1) * H], xh_wc[:, WB * k + w, :], w == 0, w == WB - 1)
                    last.then_inc(s_m, 1)

                def attend(k, r, before, after):
                    par = r % 2
                    if after(2):
                        proj_b(k + 2, r + 2)
                    if before(2):
                        sum_block(k - 2, par)
                    pe.wait_ge(s_p, NBLK * u + k + 1)
                    for w in range(WB):
                        last = nc.tensor.transpose(pt_ps[par][:, w * H:(w + 1) * H], pe_[par][:, w * H:(w + 1) * H],
                                                   ident[:])
                    last.then_inc(s_pt, 1)

                pe.wait_ge(s_y, IMG * NBAT * u + YCREDIT)
                proj_b(0, 0)
                proj_b(1, 1)
                for i in range(2):
                    pe.wait_ge(s_xh[i], 16 * NBAT // 2 * (u + 1))
                steps(pe, NBLK, RING, attend)
                for k in (NBLK - 2, NBLK - 1):
                    sum_block(k, k % 2)

                pe.wait_ge(s_xbar, u + 1)
                nc.tensor.transpose(tiny[:, 0:P], xbar[:], ident[:]).then_inc(s_xbp, 1)
                pe.wait_ge(s_xbt, u + 1)
                mm(tiny[:, P:2 * P], xbart[:], wa2[:], True).then_inc(s_gp, 1)

                def v_t(k, par):
                    pe.wait_ge(s_xb, NBLK * u + k + 1)
                    mm(vt_ps[par], ones_row[:], bv_row4[:].rearrange("a w n -> a (w n)"), True)
                    for w in range(WB):
                        last = mm(vt_ps[par][:, w * P:(w + 1) * P], xb_[par][:, w, :], wvh[:], False, True,
                                  share=True)
                    last.then_inc(s_vt, 1)

                def z(k, par):
                    pe.wait_ge(s_e, NBLK * u + k + 1)
                    pe.wait_ge(s_zn, 2 * (NBLK * u + k - 2) + 2 + ZCREDIT)
                    for w in range(WB):
                        last = mm(z_ps[par][:, w, 0:HPU * (HEAD + 1)], ev_[par][:, w * H:(w + 1) * H],
                                  gaug[:].rearrange("p h m -> p (h m)"), True)
                    last.then_inc(s_zz, 1)

                def values(k, r, before, after):
                    par = r % 2
                    mm(v_ps[par], wvs[:], xc_wh[:, bass.ts(k, WB), :], True)
                    if before(1):
                        z(k - 1, 1 - par)
                    pe.wait_ge(s_ts, NBLK * u + k + 1)
                    for w in range(WB):
                        last = mm(v_ps[par][:, w * H:(w + 1) * H],
                                  tspr[par][:, w, :, :].rearrange("p h m -> p (h m)"), nident[:], False,
                                  True, share=True)
                    last.then_inc(s_v, 1)
                    if after(2):
                        v_t(k + 2, par)

                v_t(0, 0)
                v_t(1, 1)
                pe.wait_ge(s_g, u + 1)
                steps(pe, NBLK, RING, values)
                z(NBLK - 1, 1)

                pe.wait_ge(s_gn1, u + 1)
                mm(tiny[:, 0:2 * NG], avg_p[:], mvh[:].rearrange("p g t -> p (g t)"), True).then_inc(s_gn1p, 1)

                def up_rows(g, i, par):
                    if i == 0:
                        pe.wait_ge(s_xn, g + 1)
                    else:
                        pe.wait_ge(s_t1, IMG * g + i)
                    mm3(s1_ps[:, 0:UP], xn_2[:, par, 0, i, :], xn_2[:, par, 1, i, :], up_2[:, 0, :], up_2[:, 1, :],
                        True).then_inc(s_s1, 1)

                def up_columns(g, i, par):
                    pe.wait_ge(s_y, IMG * g + i - 1 + YCREDIT)
                    for c in range(2):
                        v = slice(c * P, (c + 1) * P)
                        last = mm3(y_ps[i % 2][:, c, :], t1[:, par, 0, v, i], t1[:, par, 1, v, i], up_2[:, 0, :],
                                   up_2[:, 1, :], True)
                    last.then_inc(s_yp, 1)

                def down(o, la, lb, first):
                    mm(o[:, 0:DA], la, dn_t[:, DB - DA:DB], first, True, share=True)
                    return mm(o[:, DB0:H], lb, dn_t[:], False, True, share=True)

                def down_rows(g, i, par):
                    pe.wait_ge(s_yc, IMG * g + i + 1)
                    r, half = i % HALF, i // HALF
                    if r == HALF - 1:
                        pe.wait_ge(s_yrc, 3 * g + 3)
                    for c in range(2):
                        if r == 0:
                            pe.wait_ge(s_z1, 4 * g + 2 * half + c - 1 + DCREDIT)
                        v = slice(c * P, (c + 1) * P)
                        down(dz_ps[c][:, r * H:(r + 1) * H], yb[:, i % YRING, 0, v], yb[:, i % YRING, 1, v], r == 0)
                        if r == HALF - 1:
                            o = dz_ps[c].rearrange("p (r h) -> p r h", h=H)[:, :, H - DR:H]
                            mm(o, yr[:, par, v], dn_r[:, half * HALF:(half + 1) * HALF, :], False,
                               True, share=True).then_inc(s_dz, 1)

                def down_columns(g, half):
                    pe.wait_ge(s_z1, 4 * g + 2 * half + 2 + DCREDIT)
                    pe.wait_ge(s_zr, g + 1 + ONE)
                    pe.wait_ge(s_o, 2 * g + half + OCREDIT)
                    for r in range(HALF):
                        o = o_ps[:, r * W:(r + 1) * W]
                        a, b = ([z1[:, half, i, c, r, :] for i in range(2)] for c in range(2))
                        mm3(o[:, 0:DA], *a, dn_2[:, 0, DB - DA:DB], dn_2[:, 1, DB - DA:DB], r == 0)
                        mm3(o[:, DB0:H], *b, dn_2[:, 0, :], dn_2[:, 1, :], False)
                    o = o_ps.rearrange("p (r w) -> p r w", w=W)[:, :, W - DR:W]
                    q = slice(half * HALF, (half + 1) * HALF)
                    mm3(o, zr[:, 0, :], zr[:, 1, :], dr_2[:, 0, q, :], dr_2[:, 1, q, :], False).then_inc(s_op, 1)

                def remainder_rows(g, par):
                    pe.wait_ge(s_t1, IMG * (g + 1))
                    high, low = (t1[:, par, i, 2 * P:UP, :].rearrange("p q i -> p (q i)") for i in range(2))
                    mm3(o_ps[0:RR, 0:UP], high, low, up_2[:, 0, :], up_2[:, 1, :], True).then_inc(s_yrp, 1)

                def remainder_columns(g, par):
                    down(o_ps[0:RR, :], yc[:, par, 0, :, :].rearrange("p q i -> p (q i)"),
                         yc[:, par, 1, :, :].rearrange("p q i -> p (q i)"), True)
                    mm(o_ps[0:RR, H - DR:H], yrb[:, par, :, :].rearrange("p q i -> p (q i)"), dn_rs[:], False, True,
                       share=True).then_inc(s_zrp, 1)

                def batch(j, par, before, after):
                    g = NBAT * u + j
                    for i in range(IMG):
                        up_columns(g, i, par)
                        if after(1):
                            if i == 0:
                                pe.wait_ge(s_t1, IMG * (g + 1))
                            up_rows(g + 1, i, 1 - par)
                        if i >= LAG:
                            down_rows(g, i - LAG, par)
                        elif before(1):
                            down_rows(g - 1, IMG + i - LAG, 1 - par)
                        if i == 0:
                            pe.wait_ge(s_o, 2 * (g - 1 if before(1) else g) + OCREDIT)
                            remainder_rows(g, par)
                        if before(1):
                            if i == LAG - 1:
                                pe.wait_ge(s_yr, g + 1)
                                remainder_columns(g - 1, 1 - par)
                            if i in (3, 5):
                                down_columns(g - 1, i // 4)

                for i in range(IMG):
                    up_rows(NBAT * u, i, 0)
                steps(pe, NBAT, 2, batch)
                g = NBAT * (u + 1) - 1
                for i in range(IMG - LAG, IMG):
                    down_rows(g, i, 1)
                pe.wait_ge(s_o, 2 * g + OCREDIT)
                remainder_columns(g, 1)
                for half in range(2):
                    down_columns(g, half)

            pe.wait_ge(s_cst, 1)
            with pe.Fori(0, UNITS) as u:
                unit(u)


def kernel(x, L0_conv_Wa, L0_conv_ba, L0_conv_Wb, L0_conv_bb, L0_conv_Wv, L0_conv_bv, L1_conv_bias, L1_conv_up_filter,
           L1_conv_down_filter):
    import numpy as np
    import concourse.bacc as bacc
    from concourse.bass_utils import run_bass_kernel_spmd

    nc = bacc.Bacc("TRN2", target_bir_lowering=False, num_devices=1)
    host = {"x": x, "WaT": np.asarray(L0_conv_Wa).T, "ba": L0_conv_ba, "WbT": np.asarray(L0_conv_Wb).T,
            "bb": L0_conv_bb, "WvT": np.asarray(L0_conv_Wv).T, "bv": L0_conv_bv, "bias": L1_conv_bias, "fup": L1_conv_up_filter,
            "fdn": L1_conv_down_filter}
    arrays, args = {}, []
    for name, a in host.items():
        a = np.ascontiguousarray(a)
        arrays["in_" + name] = a
        args.append(nc.dram_tensor("in_" + name, a.shape, mybir.dt.from_np(a.dtype), kind="ExternalInput").ap())
    o = nc.dram_tensor("out_0", (B, C, H, W), mybir.dt.float32, kind="ExternalOutput").ap()
    attention_then_filters(nc, *args, o)
    r = run_bass_kernel_spmd(nc, [arrays], core_ids=[0])
    return r.results[0]["out_0"]
```
